# Optimizing a Trainium2 kernel written in Bass

```python
import numpy as np
import jax
import jax.numpy as jnp

def _softmax(x, axis=-1):
    return jax.nn.softmax(x, axis=axis)

def _gelu(x):
    return jax.nn.gelu(x, approximate=True)

def _silu(x):
    return jax.nn.silu(x)

def _sigmoid(x):
    return jax.nn.sigmoid(x)

def _layernorm(x, axis=-1, eps=1e-05):
    m = jnp.mean(x, axis=axis, keepdims=True)
    v = jnp.var(x, axis=axis, keepdims=True)
    return (x - m) / jnp.sqrt(v + eps)

def _scatter_add(tgt, idx, src, axis=0):
    return tgt.at[idx].add(src)

def _segment_sum(src, seg, n):
    return jax.ops.segment_sum(src, seg, n)
kernel_name = 'mk_macaron_d1_jaxref_r8_24dc01'

def setup_inputs(seed: int=0):
    np.random.seed(seed)
    _w = jnp.asarray

    def _L0_attn_setup():
        import jax, jax.numpy as jnp
        import numpy as np
        B, S, D_IN = (4, 256, 128)
        D_Q = D_K = D_V = 128
        key = jax.random.key(seed)
        ks = jax.random.split(key, 6)
        s = lambda d: 1.0 / np.sqrt(d)
        return {'x': jax.random.normal(ks[0], (B, S, D_IN), dtype=jnp.float32), 'Wk': jax.random.normal(ks[1], (D_K, D_IN), dtype=jnp.float32) * s(D_IN), 'Wq': jax.random.normal(ks[2], (D_Q, D_IN), dtype=jnp.float32) * s(D_IN), 'Wv': jax.random.normal(ks[3], (D_V, D_IN), dtype=jnp.float32) * s(D_IN), 'Wa': jax.random.normal(ks[4], (D_Q, D_K), dtype=jnp.float32) * s(D_K), 'Wb': jax.random.normal(ks[5], (D_V, D_V), dtype=jnp.float32) * s(D_V)}
    _L0_attn_in = _L0_attn_setup()

    def _L0_ffn_setup():
        import jax, jax.numpy as jnp
        import numpy as np
        DIM = 128
        DEPTH = 6
        HEADS = 16
        DIM_HEAD = 64
        WINDOW = 32
        INNER = HEADS * DIM_HEAD
        DIM_INNER = int(DIM * 4 * 2 / 3)
        QK_SCALE = 8.0

        def shift_tokens(t):
            a, s = jnp.split(t, 2, -1)
            s = jnp.pad(s, ((0, 0), (1, 0), (0, 0)))[:, :-1]
            return jnp.concatenate([a, s], -1)

        def l2norm(t):
            return t / jnp.maximum(jnp.linalg.norm(t, axis=-1, keepdims=True), 1e-12)

        def rotate_half(x):
            x1, x2 = jnp.split(x, 2, -1)
            return jnp.concatenate([-x2, x1], -1)

        def rotary_tables(n):
            half = jnp.arange(0, DIM_HEAD, 2, dtype=jnp.float32)
            inv_freq = 1.0 / 10000.0 ** (half / DIM_HEAD)
            t = jnp.arange(n, dtype=jnp.float32)
            freqs = t[:, None] * inv_freq[None, :]
            freqs = jnp.concatenate([freqs, freqs], -1)
            base_scale = (half + 0.4 * DIM_HEAD) / (1.4 * DIM_HEAD)
            power = (t - n // 2) / (WINDOW // 2)
            scale = base_scale[None, :] ** power[:, None]
            scale = jnp.concatenate([scale, scale], -1)
            return (freqs, scale)

        def local_attention(q, k, v):
            b, h, n, d = q.shape
            w = WINDOW
            nw = n // w
            bq = q.reshape(b, h, nw, w, d)
            bk = k.reshape(b, h, nw, w, d)
            bv = v.reshape(b, h, nw, w, d)

            def look(t):
                p = jnp.pad(t, ((0, 0), (0, 0), (1, 0), (0, 0), (0, 0)))
                return jnp.concatenate([p[:, :, :nw], p[:, :, 1:]], axis=3)
            bk2, bv2 = (look(bk), look(bv))
            seq = jnp.arange(n).reshape(nw, w)
            seq_p = jnp.pad(seq, ((1, 0), (0, 0)), constant_values=-1)
            jt = jnp.concatenate([seq_p[:nw], seq_p[1:]], axis=1)
            it = seq[:, :, None]
            jb = jt[:, None, :]
            mask = (it < jb) | (it > jb + w) | (jb == -1)
            sim = jnp.einsum('bhwie,bhwje->bhwij', bq, bk2) * QK_SCALE
            sim = jnp.where(mask, -jnp.finfo(sim.dtype).max, sim)
            attn = jax.nn.softmax(sim, -1)
            out = jnp.einsum('bhwij,bhwje->bhwie', attn, bv2)
            return out.reshape(b, h, n, d)

        def attn_layer(x, Wqkv, qs, ksc, Wo):
            b, n, _ = x.shape
            qkv = x @ Wqkv
            q, k, v = jnp.split(qkv, 3, -1)
            sh = lambda t: t.reshape(b, n, HEADS, DIM_HEAD).transpose(0, 2, 1, 3)
            q, k, v = (sh(q), sh(k), sh(v))
            q = l2norm(q) * qs
            k = l2norm(k) * ksc
            freqs, scale = rotary_tables(n)
            cos, sin = (jnp.cos(freqs), jnp.sin(freqs))
            q = q * cos * scale + rotate_half(q) * sin * scale
            inv = 1.0 / scale
            k = k * cos * inv + rotate_half(k) * sin * inv
            out = local_attention(q, k, v)
            out = out.transpose(0, 2, 1, 3).reshape(b, n, INNER)
            return out @ Wo

        def ffn_layer(x, g, bln, W1, b1, W2, b2):
            mu = x.mean(-1, keepdims=True)
            var = ((x - mu) ** 2).mean(-1, keepdims=True)
            xn = (x - mu) / jnp.sqrt(var + 1e-05) * g + bln
            hg = xn @ W1 + b1
            a, gate = jnp.split(hg, 2, -1)
            return a * jax.nn.gelu(gate, approximate=False) @ W2 + b2
        key = jax.random.key(seed)
        ks = jax.random.split(key, 8)
        B, N = (2, 256)
        init = lambda k, shape: jax.random.normal(k, shape, jnp.float32) * 0.02
        return {'x': jax.random.normal(ks[0], (B, N, DIM), jnp.float32), 'Wqkv': init(ks[1], (DEPTH, DIM, 3 * INNER)), 'q_scale': jnp.ones((DEPTH, DIM_HEAD), jnp.float32), 'k_scale': jnp.ones((DEPTH, DIM_HEAD), jnp.float32), 'Wo': init(ks[2], (DEPTH, INNER, DIM)), 'ln_g': jnp.ones((DEPTH, DIM), jnp.float32), 'ln_b': jnp.zeros((DEPTH, DIM), jnp.float32), 'W1': init(ks[3], (DEPTH, DIM, 2 * DIM_INNER)), 'b1': jnp.zeros((DEPTH, 2 * DIM_INNER), jnp.float32), 'W2': init(ks[4], (DEPTH, DIM_INNER, DIM)), 'b2': jnp.zeros((DEPTH, DIM), jnp.float32)}
    _L0_ffn_in = _L0_ffn_setup()
    _d = {'L0_attn_x': _L0_attn_in['x'], 'L0_attn_Wk': _L0_attn_in['Wk'], 'L0_attn_Wq': _L0_attn_in['Wq'], 'L0_attn_Wv': _L0_attn_in['Wv'], 'L0_attn_Wa': _L0_attn_in['Wa'], 'L0_attn_Wb': _L0_attn_in['Wb'], 'L0_ffn_Wqkv': _L0_ffn_in['Wqkv'], 'L0_ffn_q_scale': _L0_ffn_in['q_scale'], 'L0_ffn_k_scale': _L0_ffn_in['k_scale'], 'L0_ffn_Wo': _L0_ffn_in['Wo'], 'L0_ffn_ln_g': _L0_ffn_in['ln_g'], 'L0_ffn_ln_b': _L0_ffn_in['ln_b'], 'L0_ffn_W1': _L0_ffn_in['W1'], 'L0_ffn_b1': _L0_ffn_in['b1'], 'L0_ffn_W2': _L0_ffn_in['W2'], 'L0_ffn_b2': _L0_ffn_in['b2']}
    _x0 = _d['L0_attn_x']
    _d['L0_attn_x'] = jax.random.normal(jax.random.fold_in(jax.random.key(seed), 1), (4, 512, 128), dtype=_x0.dtype)
    del _x0
    return _d

def reference(L0_attn_x, L0_attn_Wk, L0_attn_Wq, L0_attn_Wv, L0_attn_Wa, L0_attn_Wb, L0_ffn_Wqkv, L0_ffn_q_scale, L0_ffn_k_scale, L0_ffn_Wo, L0_ffn_ln_g, L0_ffn_ln_b, L0_ffn_W1, L0_ffn_b1, L0_ffn_W2, L0_ffn_b2):

    def _L0_attn_ref(x, Wk, Wq, Wv, Wa, Wb):
        import jax, jax.numpy as jnp
        import numpy as np
        B, S, D_IN = (4, 256, 128)
        D_Q = D_K = D_V = 128
        k = jnp.einsum('bsd,kd->bsk', x, Wk)
        q = jnp.einsum('bsd,qd->bsq', x, Wq)
        v = jnp.einsum('bsd,vd->bsv', x, Wv)
        ak = jnp.einsum('bsk,qk->bsq', k, Wa)
        e = jnp.einsum('biq,bjq->bij', q, ak)
        alpha = jax.nn.softmax(e, axis=-1)
        u = jnp.einsum('bsv,wv->bsw', v, Wb)
        out = jnp.einsum('bij,bjv->biv', alpha, u)
        return out

    def _L0_ffn_ref(x, Wqkv, q_scale, k_scale, Wo, ln_g, ln_b, W1, b1, W2, b2):
        import jax, jax.numpy as jnp
        import numpy as np
        DIM = 128
        DEPTH = 6
        HEADS = 16
        DIM_HEAD = 64
        WINDOW = 32
        INNER = HEADS * DIM_HEAD
        DIM_INNER = int(DIM * 4 * 2 / 3)
        QK_SCALE = 8.0

        def shift_tokens(t):
            a, s = jnp.split(t, 2, -1)
            s = jnp.pad(s, ((0, 0), (1, 0), (0, 0)))[:, :-1]
            return jnp.concatenate([a, s], -1)

        def l2norm(t):
            return t / jnp.maximum(jnp.linalg.norm(t, axis=-1, keepdims=True), 1e-12)

        def rotate_half(x):
            x1, x2 = jnp.split(x, 2, -1)
            return jnp.concatenate([-x2, x1], -1)

        def rotary_tables(n):
            half = jnp.arange(0, DIM_HEAD, 2, dtype=jnp.float32)
            inv_freq = 1.0 / 10000.0 ** (half / DIM_HEAD)
            t = jnp.arange(n, dtype=jnp.float32)
            freqs = t[:, None] * inv_freq[None, :]
            freqs = jnp.concatenate([freqs, freqs], -1)
            base_scale = (half + 0.4 * DIM_HEAD) / (1.4 * DIM_HEAD)
            power = (t - n // 2) / (WINDOW // 2)
            scale = base_scale[None, :] ** power[:, None]
            scale = jnp.concatenate([scale, scale], -1)
            return (freqs, scale)

        def local_attention(q, k, v):
            b, h, n, d = q.shape
            w = WINDOW
            nw = n // w
            bq = q.reshape(b, h, nw, w, d)
            bk = k.reshape(b, h, nw, w, d)
            bv = v.reshape(b, h, nw, w, d)

            def look(t):
                p = jnp.pad(t, ((0, 0), (0, 0), (1, 0), (0, 0), (0, 0)))
                return jnp.concatenate([p[:, :, :nw], p[:, :, 1:]], axis=3)
            bk2, bv2 = (look(bk), look(bv))
            seq = jnp.arange(n).reshape(nw, w)
            seq_p = jnp.pad(seq, ((1, 0), (0, 0)), constant_values=-1)
            jt = jnp.concatenate([seq_p[:nw], seq_p[1:]], axis=1)
            it = seq[:, :, None]
            jb = jt[:, None, :]
            mask = (it < jb) | (it > jb + w) | (jb == -1)
            sim = jnp.einsum('bhwie,bhwje->bhwij', bq, bk2) * QK_SCALE
            sim = jnp.where(mask, -jnp.finfo(sim.dtype).max, sim)
            attn = jax.nn.softmax(sim, -1)
            out = jnp.einsum('bhwij,bhwje->bhwie', attn, bv2)
            return out.reshape(b, h, n, d)

        def attn_layer(x, Wqkv, qs, ksc, Wo):
            b, n, _ = x.shape
            qkv = x @ Wqkv
            q, k, v = jnp.split(qkv, 3, -1)
            sh = lambda t: t.reshape(b, n, HEADS, DIM_HEAD).transpose(0, 2, 1, 3)
            q, k, v = (sh(q), sh(k), sh(v))
            q = l2norm(q) * qs
            k = l2norm(k) * ksc
            freqs, scale = rotary_tables(n)
            cos, sin = (jnp.cos(freqs), jnp.sin(freqs))
            q = q * cos * scale + rotate_half(q) * sin * scale
            inv = 1.0 / scale
            k = k * cos * inv + rotate_half(k) * sin * inv
            out = local_attention(q, k, v)
            out = out.transpose(0, 2, 1, 3).reshape(b, n, INNER)
            return out @ Wo

        def ffn_layer(x, g, bln, W1, b1, W2, b2):
            mu = x.mean(-1, keepdims=True)
            var = ((x - mu) ** 2).mean(-1, keepdims=True)
            xn = (x - mu) / jnp.sqrt(var + 1e-05) * g + bln
            hg = xn @ W1 + b1
            a, gate = jnp.split(hg, 2, -1)
            return a * jax.nn.gelu(gate, approximate=False) @ W2 + b2
        for i in range(DEPTH):
            x = attn_layer(shift_tokens(x), Wqkv[i], q_scale[i], k_scale[i], Wo[i]) + x
            x = ffn_layer(shift_tokens(x), ln_g[i], ln_b[i], W1[i], b1[i], W2[i], b2[i]) + x
        return x
    x = L0_attn_x
    x = x + 0.5 * _L0_ffn_ref(_layernorm(x, axis=-1), L0_ffn_Wqkv, L0_ffn_q_scale, L0_ffn_k_scale, L0_ffn_Wo, L0_ffn_ln_g, L0_ffn_ln_b, L0_ffn_W1, L0_ffn_b1, L0_ffn_W2, L0_ffn_b2)
    x = x + _L0_attn_ref(_layernorm(x, axis=-1), L0_attn_Wk, L0_attn_Wq, L0_attn_Wv, L0_attn_Wa, L0_attn_Wb)
    x = x + 0.5 * _L0_ffn_ref(_layernorm(x, axis=-1), L0_ffn_Wqkv, L0_ffn_q_scale, L0_ffn_k_scale, L0_ffn_Wo, L0_ffn_ln_g, L0_ffn_ln_b, L0_ffn_W1, L0_ffn_b1, L0_ffn_W2, L0_ffn_b2)
    return x

_drawn_inputs = setup_inputs


def setup_inputs(seed=0):
    import zlib

    import numpy as np

    out = dict(_drawn_inputs(seed))
    spreads = {'L0_ffn_q_scale': (1.0, 0.6),
     'L0_ffn_k_scale': (1.0, 0.6),
     'L0_ffn_ln_g': (1.0, 0.6),
     'L0_ffn_ln_b': (0.0, 0.8),
     'L0_ffn_b1': (0.0, 0.527),
     'L0_ffn_b2': (0.0, 0.1)}
    factors = {}
    for name, (base, spread) in spreads.items():
        noise = np.random.default_rng([zlib.crc32(name.encode()), seed]).standard_normal(out[name].shape)
        drawn = base * np.exp(spread * noise) if base else spread * noise
        out[name] = jnp.asarray(drawn.astype(out[name].dtype))
    for name, factor in factors.items():
        out[name] = (out[name] * factor).astype(out[name].dtype)
    return out
```

```python
from contextlib import ExitStack

import concourse.bass as bass
from concourse import mybir

F32 = mybir.dt.float32
BF16 = mybir.dt.bfloat16
ALU = mybir.AluOpType
ACT = mybir.ActivationFunctionType
AX_X = mybir.AxisListType.X

P = 128
B, S, D = 4, 512, 128
LAYERS, HEADS, DH, WIN = 6, 16, 64, 32
HALF = DH // 2
GH = P // HALF
GROUPS = HEADS // GH
TILES = S // P
WPT = P // WIN
PAIRS = HEADS // 2
FF = D * 4 * 2 // 3
CHUNKS = [(c, min(P, FF - c)) for c in range(0, FF, P)]
NC = len(CHUNKS)
ITERS = LAYERS * B
SPAN = P + WIN
QK_SCALE = 8.0
LN_EPS = 1e-5
NORM_EPS = 1e-12
MASKED = -1e30
VEC = 6 + 2 * NC + 1


def need(eng, sem, count):
    if not isinstance(count, int) or count > 0:
        eng.wait_ge(sem, count)


def macaron(nc, x_t, w_qk, w_v, w_o, w_1, w_2, vec, rot, mask, ident, a_w, sel, out):
    with ExitStack() as ctx:
        def sb(name, shape, dt=F32):
            return ctx.enter_context(nc.sbuf_tensor(name, shape, dt))

        def ps(name, shape):
            return ctx.enter_context(nc.psum_tensor(name, shape, F32))

        def sem(name):
            return ctx.enter_context(nc.semaphore(name))

        X = sb("X", [P, B, S])
        Z = sb("Z", [P, B, S])
        wqk = sb("wqk", [P, GROUPS, 4, P])
        wv = sb("wv", [P, HEADS * DH])
        wo = sb("wo", [P, PAIRS, D])
        w1 = sb("w1", [P, 2 * FF])
        w2 = sb("w2", [P, NC, D])
        attn_w = sb("attn_w", [P, 5, D])
        vecs = sb("vecs", [P, LAYERS, VEC])
        vqk = sb("vqk", [P, 4])
        vff = sb("vff", [P, VEC - 4])
        rotary = sb("rotary", [P, 4, S])
        cq, sq_, ck, sk = (rotary[:, i, :] for i in range(4))
        identity = sb("identity", [P, P])
        identity16 = sb("identity16", [P, P], BF16)
        mask16 = sb("mask16", [P, 2, 2 * GH * 2 * WIN], BF16)
        head_sel = sb("head_sel", [P, WIN])
        mean_w = sb("mean_w", [P, P])
        xs = sb("xs", [P, S])
        squares = sb("squares", [P, 4, S])
        sumsq = sb("sumsq", [P, 2, S])
        q_terms = sb("q_terms", [P, 4, S])
        k_terms = sb("k_terms", [P, 4, S])
        q_rotated = sb("q_rotated", [P, 2, 2, S])
        k_rotated = sb("k_rotated", [P, 2, S])
        k_normed = sb("k_normed", [P, 2, S])
        khat = sb("khat", [P, 2, GH, WIN + S])
        tok_sums = sb("tok_sums", [P, 2 * TILES, WIN])
        norm2 = sb("norm2", [P, 2 * TILES * GH])
        inv2 = sb("inv2", [P, 2 * TILES * GH])
        inv_q = sb("inv_q", [P, 2, TILES * GH])
        inv_k = sb("inv_k", [P, TILES * GH, HALF])
        row_max = sb("row_max", [P, TILES * GH])
        row_sum = sb("row_sum", [P, TILES * GH])
        inv_sum = sb("inv_sum", [P, TILES * GH])
        probs = sb("probs", [P, TILES * GH, 2 * WIN])
        probs_t = sb("probs_t", [P, TILES, GH, 2, WIN])
        band = sb("band", [P, TILES, GH, SPAN])
        V = sb("V", [P, TILES, HEADS * DH])
        heads_out = sb("heads_out", [P, PAIRS, S])
        z_mid = sb("z_mid", [P, S])
        z_shift = sb("z_shift", [P, S])
        centred = sb("centred", [P, S])
        ln_sq = sb("ln_sq", [P, S])
        ln_var = sb("ln_var", [P, TILES])
        ln_inv = sb("ln_inv", [P, TILES])
        ln_rstd = sb("ln_rstd", [P, TILES, P])
        ln_out = sb("ln_out", [P, S])
        ln_aff = sb("ln_aff", [P, S])
        gate = sb("gate", [P, NC, S])
        hidden = sb("hidden", [P, NC, S])

        primer = sb("primer", [P, 3])

        p4 = ps("p4", [P, 4, S])
        pq, pk = p4[:, 0:2, :], p4[:, 2:4, :]
        pS = ps("pS", [P, 2, S])
        pO = ps("pO", [P, S])
        pM = ps("pM", [P, S])

        consts_in, consts_cast, cleared = sem("consts_in"), sem("consts_cast"), sem("cleared")
        wqk_in = [sem(f"wqk_in{g}") for g in range(GROUPS)]
        wv_in, wo_in, wff_in = sem("wv_in"), sem("wo_in"), sem("wff_in")
        xs_ready = sem("xs_ready")
        q_proj, k_proj, squared, paired = sem("q_proj"), sem("k_proj"), sem("squared"), sem("paired")
        q_prod, k_prod, q_rot, k_rot = sem("q_prod"), sem("k_prod"), sem("q_rot"), sem("k_rot")
        summed, by_token, clamped, inverted, rooted = (
            sem("summed"), sem("by_token"), sem("clamped"), sem("inverted"), sem("rooted"))
        spread_k, k_norm, khat_in = sem("spread_k"), sem("k_norm"), sem("khat_in")
        scored, maxed, shifted, scaled, expd = (sem("scored"), sem("maxed"), sem("shifted"), sem("scaled"), sem("expd"))
        rows_summed, sums_inverted, normed = sem("rows_summed"), sem("sums_inverted"), sem("normed")
        transposed, placed, valued, o_saved = sem("transposed"), sem("placed"), sem("valued"), sem("o_saved")
        v_proj, v_saved = sem("v_proj"), sem("v_saved")
        vqk_set, vff_set = sem("vqk_set"), sem("vff_set")
        o_proj, z_mid_set, z_shifted = sem("o_proj"), sem("z_mid_set"), sem("z_shifted")
        mean_done, centred_set, ln_squared, var_done = (sem("mean_done"), sem("centred_set"), sem("ln_squared"), sem("var_done"))
        var_eps, var_inverted, rstd_set, rstd_spread = (sem("var_eps"), sem("var_inverted"), sem("rstd_set"), sem("rstd_spread"))
        ln_scaled, ln_done = sem("ln_scaled"), sem("ln_done")
        gates_up, values_up, gelu_done, hidden_set = (sem("gates_up"), sem("values_up"), sem("gelu_done"), sem("hidden_set"))
        ff_down, z_done = sem("ff_down"), sem("z_done")
        n_mean, n_centred, n_squared, n_var, n_eps, n_inv, n_rstd, n_spread, n_done = (
            sem("n_" + s) for s in ("mean", "centred", "squared", "var", "eps", "inv", "rstd", "spread", "done"))
        x_updated = sem("x_updated")
        a_kqv, a_k, a_v, a_q, a_ak, a_u, a_aks, a_us, a_scores, a_max, a_exp = (
            sem("a_" + s) for s in ("kqv", "k", "v", "q", "ak", "u", "aks", "us", "scores", "max", "exp"))
        a_sum, a_isum, a_norm, a_tr, a_trs, a_trd, a_out, a_done = (
            sem("a_" + s) for s in ("sum", "isum", "norm", "tr", "trs", "trd", "out", "done"))
        out_stored = sem("out_stored")

        block = ctx.enter_context(nc.Block())
        CONSTS = 7 * 16

        def has(g, back, prev, cur):
            return cur if g >= back else prev

        def batch(t, n):
            return t[:, bass.ds(n % B, 1), :].rearrange("p a s -> p (a s)")

        def emit(body, eng, n0):
            body(n0, prev=False, cur=True)
            with eng.Fori(n0 + 1, n0 + ITERS) as n:
                body(n, prev=True, cur=True)
            body(n0 + ITERS, prev=True, cur=False)

        @block.sync
        def _(sp):
            for dst, src in ((X[:], x_t), (vecs[:], vec), (rotary[:], rot), (identity[:], ident),
                             (squares[:, 0:2, :], mask), (head_sel[:], sel),
                             (attn_w[:].rearrange("p a m -> p (a m)"), a_w)):
                sp.dma_start(dst, src).then_inc(consts_in, 16)

            def load_qk(layer, g):
                sp.dma_start(wqk[:, g, :, :].rearrange("p a m -> p (a m)"),
                             w_qk[bass.ds(layer, 1), g, :, :].rearrange("a p m -> p (a m)")).then_inc(wqk_in[g], 16)

            def load_v(layer):
                sp.dma_start(wv[:], w_v[bass.ds(layer, 1), :, :].rearrange("a p m -> p (a m)")).then_inc(wv_in, 16)

            def load_o(layer):
                sp.dma_start(wo[:].rearrange("p a m -> p (a m)"),
                             w_o[bass.ds(layer, 1), :, :].rearrange("a p m -> p (a m)")).then_inc(wo_in, 16)

            def load_ff(layer):
                sp.dma_start(w1[:], w_1[bass.ds(layer, 1), :, :].rearrange("a p m -> p (a m)")).then_inc(wff_in, 16)
                sp.dma_start(w2[:].rearrange("p a m -> p (a m)"),
                             w_2[bass.ds(layer, 1), :, :].rearrange("a p m -> p (a m)")).then_inc(wff_in, 16)

            for g in range(GROUPS):
                load_qk(0, g)
            load_v(0)
            load_o(0)
            load_ff(0)
            sp.wait_ge(cleared, 5)

            def spread(u):
                need(sp, k_norm, u + 1)
                for h in range(GH):
                    sp.dma_start(khat[HALF * h:HALF * (h + 1), :, h, WIN:],
                                 k_normed[HALF * h:HALF * (h + 1), :, :]).then_inc(khat_in, 16)

            def layer_loads(lay, first, last):
                for row in range(B):
                    for g in range(GROUPS):
                        spread(4 * (B * lay + row) + g)
                        if row == 0 and g == 3 and not first:
                            load_o(lay % LAYERS)
                        if row == 1 and g == 0 and not first:
                            load_ff(lay % LAYERS)
                        if row == B - 1 and not last:
                            load_qk((lay + 1) % LAYERS, g)
                            if g == 3:
                                load_v((lay + 1) % LAYERS)

            layer_loads(0, True, False)
            with sp.Fori(1, 2 * LAYERS - 1) as lay:
                layer_loads(lay, False, False)
            layer_loads(2 * LAYERS - 1, False, True)
            sp.wait_ge(x_updated, 2)
            sp.dma_start(out, X[:]).then_inc(out_stored, 16)
            sp.wait_ge(out_stored, 16)

        @block.tensor
        def _(pe):
            mm = nc.tensor.matmul
            pe.wait_ge(consts_in, CONSTS)
            pe.wait_ge(consts_cast, 2)
            pe.wait_ge(cleared, 5)

            def layer_norm(k, src):
                need(pe, n_done, k + 1)
                mm(pM[:], mean_w[:], src, start=True, stop=True).then_inc(n_mean, 1)
                need(pe, n_squared, k + 1)
                for j in range(TILES):
                    last = mm(pM[:, j:j + 1], ln_sq[:, P * j:P * (j + 1)], mean_w[:, 0:1], start=True, stop=True)
                last.then_inc(n_var, 1)
                need(pe, n_rstd, k + 1)
                for j in range(TILES):
                    last = mm(pM[:, P * j:P * (j + 1)], ln_rstd[:, j, :], identity[:], start=True, stop=True)
                last.then_inc(n_spread, 1)

            def attention(b):
                wk_, wq_, wv_, wa_, wb_ = (attn_w[:, i, :] for i in range(5))
                need(pe, a_done, b + 1)
                mm(p4[:, 0, :], wk_, batch(Z, b), start=True, stop=True)
                mm(p4[:, 1, :], wq_, batch(Z, b), start=True, stop=True)
                mm(p4[:, 2, :], wv_, batch(Z, b), start=True, stop=True).then_inc(a_kqv, 1)
                need(pe, a_k, b + 1)
                mm(p4[:, 3, :], wa_, squares[:, 0, :], start=True, stop=True).then_inc(a_ak, 1)
                need(pe, a_v, b + 1)
                for j in range(TILES):
                    last = mm(pO[:, P * j:P * (j + 1)], squares[:, 2, P * j:P * (j + 1)], wb_, start=True, stop=True)
                last.then_inc(a_u, 1)
                need(pe, a_aks, b + 1)
                need(pe, a_q, b + 1)
                for i in range(TILES):
                    last = mm(p4[:, i, :], squares[:, 1, P * i:P * (i + 1)], squares[:, 3, :], start=True, stop=True)
                last.then_inc(a_scores, 1)
                need(pe, a_norm, b + 1)
                for j in range(TILES):
                    for i in range(TILES):
                        last = mm(p4[:, j, P * i:P * (i + 1)], q_terms[:, i, P * j:P * (j + 1)], identity[:],
                                  start=True, stop=True)
                last.then_inc(a_tr, 1)
                need(pe, a_trs, b + 1)
                need(pe, a_trd, b + 1)
                need(pe, a_us, b + 1)
                for j in range(TILES):
                    last = mm(pS[:, 0, :], sumsq[:, 0, P * j:P * (j + 1)], k_terms[:, j, :],
                              start=(j == 0), stop=(j == TILES - 1))
                last.then_inc(a_out, 1)

            def body(n, prev, cur, st):
                for g in range(GROUPS):
                    u = 4 * n + g
                    if cur:
                        need(pe, xs_ready, n + 1 + st)
                        need(pe, wqk_in[g], 16 * (n // B + 1))
                        need(pe, k_prod, u)
                        mm(pk[:, 0, :], wqk[:, g, 2, :], xs[:], start=True, stop=True)
                        mm(pk[:, 1, :], wqk[:, g, 3, :], xs[:], start=True, stop=True).then_inc(k_proj, 1)
                        need(pe, q_prod, u)
                        mm(pq[:, 0, :], wqk[:, g, 0, :], xs[:], start=True, stop=True)
                        mm(pq[:, 1, :], wqk[:, g, 1, :], xs[:], start=True, stop=True).then_inc(q_proj, 1)

                    def values(pair):
                        need(pe, o_saved, 2 * (u - 3) + pair)
                        if pair == 0:
                            need(pe, placed, u - 2)
                            need(pe, v_saved, 2 * TILES * (n + 1 if g == 3 else n))
                        for hh in range(2):
                            h = 2 * pair + hh
                            feat = (GH * ((g - 3) % GROUPS) + h) * DH
                            for j in range(TILES):
                                wide = min(SPAN, S - P * j)
                                last = mm(pO[DH * hh:DH * (hh + 1), P * j:P * j + wide],
                                          V[:, j, feat:feat + DH], band[:, j, h, 0:wide],
                                          start=(j == 0), stop=(j == TILES - 1), skip_group_check=True)
                        last.then_inc(valued, 1)

                    def scores(half):
                        qr = q_rotated[:, (g - 1) % 2, :, :]
                        mm(pS[:, half, :], identity16[:], mask16[:, half, :], start=True, stop=False,
                           skip_group_check=True)
                        for j in range(2):
                            cols = j * GH * 2 * WIN
                            for ab in range(2):
                                for q in range(WPT):
                                    w = WPT * (2 * half + j) + q
                                    last = mm(pS[WIN * q:WIN * (q + 1), half, cols:cols + GH * 2 * WIN],
                                              qr[:, ab, WIN * w:WIN * (w + 1)],
                                              khat[:, ab, :, WIN * w:WIN * (w + 2)],
                                              start=False, stop=(ab == 1), skip_group_check=True)
                        return last

                    if has(g, 3, prev, cur):
                        values(0)
                    if g == 3 and prev:
                        need(pe, ln_squared, n)
                        need(pe, centred_set, n)
                        for j in range(TILES):
                            last = mm(pM[:, j:j + 1], ln_sq[:, P * j:P * (j + 1)], mean_w[:, 0:1], start=True, stop=True)
                        last.then_inc(var_done, 1)
                    if has(g, 3, prev, cur):
                        values(1)
                    if cur:
                        need(pe, paired, 2 * u + 2)
                        need(pe, k_norm, u)
                        if g == 0:
                            need(pe, z_done, n)
                        if g == 3 and prev:
                            need(pe, var_eps, n)
                        if g == 3 and not prev:
                            need(pe, v_saved, 2 * TILES * (n + 1))
                        for qk in range(2):
                            by_window = sumsq[:, qk, :].rearrange("p (j q t) -> p j q t", j=TILES, q=WPT)
                            for q in range(WPT):
                                last = mm(pM[WIN * q:WIN * (q + 1), P * qk:P * (qk + 1)], head_sel[:],
                                          by_window[:, :, q, :], start=True, stop=True, skip_group_check=True)
                        last.then_inc(summed, 1)
                    if has(g, 1, prev, cur):
                        need(pe, shifted, u - 1)
                        need(pe, q_rot, u)
                        need(pe, khat_in, 16 * GH * u)
                        scores(0)
                    if g == 3 and prev:
                        need(pe, rstd_set, n)
                        if cur:
                            need(pe, by_token, u + 1)
                        for j in range(TILES):
                            last = mm(pM[:, P * j:P * (j + 1)], ln_rstd[:, j, :], identity[:], start=True, stop=True)
                        last.then_inc(rstd_spread, 1)
                    if has(g, 1, prev, cur):
                        scores(1).then_inc(scored, 1)
                    if cur:
                        need(pe, rooted, u + 1)
                        if g == 3 and prev:
                            need(pe, ln_scaled, n)
                        for j in range(TILES):
                            last = mm(pM[:, P * j:P * (j + 1)],
                                      inv_k[:, GH * j:GH * (j + 1), :].rearrange("p h d -> p (h d)"),
                                      identity[:], start=True, stop=True)
                        last.then_inc(spread_k, 1)
                    if g == 2 and prev:
                        need(pe, wo_in, 16 * ((n - 1) // B + 1))
                        need(pe, o_saved, 8 * n)
                        for i in range(PAIRS):
                            last = mm(pO[:], wo[:, i, :], heads_out[:, i, :], start=(i == 0), stop=(i == PAIRS - 1))
                        last.then_inc(o_proj, 1)
                    if g == 2 and cur:
                        need(pe, wv_in, 16 * (n // B + 1))
                        need(pe, k_norm, u + 1)
                        for c in range(2 * TILES):
                            j, half = divmod(c, 2)
                            if c == 1 and prev:
                                need(pe, z_mid_set, n)
                            if c >= 2:
                                need(pe, v_saved, 2 * TILES * n + c - 1)
                            mm((pM if c % 2 == 0 else pO)[:], xs[:, P * j:P * (j + 1)], wv[:, S * half:S * (half + 1)],
                               start=True, stop=True).then_inc(v_proj, 1)
                    if g == 2 and prev:
                        need(pe, z_shifted, n)
                        if cur:
                            need(pe, v_saved, 2 * TILES * (n + 1))
                        mm(pM[:], mean_w[:], z_shift[:], start=True, stop=True).then_inc(mean_done, 1)
                    if g == 3 and prev:
                        need(pe, ln_done, n)
                        need(pe, wff_in, 32 * ((n - 1) // B + 1))
                        for c, bank in enumerate((pq[:, 0, :], pq[:, 1, :], pk[:, 0, :])):
                            if cur:
                                need(pe, q_prod if c < 2 else k_prod, u + 1)
                            f, m = CHUNKS[c]
                            mm(bank[0:m, :], w1[:, FF + f:FF + f + m], ln_aff[:], start=True, stop=True)\
                                .then_inc(gates_up, 1)
                        need(pe, o_saved, 2 * (u - 3) + 2 if cur else 8 * n)
                        if cur:
                            need(pe, k_norm, u + 1)
                        for c, bank in enumerate((pk[:, 1, :], pM[:], pO[:])):
                            f, m = CHUNKS[c]
                            mm(bank[0:m, :], w1[:, f:f + m], ln_aff[:], start=True, stop=True).then_inc(values_up, 1)
                        need(pe, hidden_set, NC * n)
                        for c in range(NC):
                            m = CHUNKS[c][1]
                            last = mm(pM[:], w2[0:m, c, :], hidden[0:m, c, :], start=(c == 0), stop=(c == NC - 1))
                        last.then_inc(ff_down, 1)

            with pe.Fori(0, B) as b:
                layer_norm(b, batch(X, b))
            emit(lambda n, prev, cur: body(n, prev, cur, 0), pe, 0)
            pe.wait_ge(x_updated, 1)
            with pe.Fori(0, B) as b:
                layer_norm(B + b, batch(X, b))
            pe.wait_ge(n_done, 2 * B + 1)
            with pe.Fori(0, B) as b:
                attention(b)
            pe.wait_ge(a_done, B + 1)
            with pe.Fori(0, B) as b:
                layer_norm(2 * B + b, batch(X, b))
            emit(lambda n, prev, cur: body(n, prev, cur, 1), pe, ITERS)

        @block.scalar
        def _(act):
            run = nc.scalar.activation
            act.wait_ge(cleared, 5)

            def layer_norm(k):
                need(act, n_centred, k + 1)
                run(ln_sq[:], centred[:], ACT.Square).then_inc(n_squared, 1)
                need(act, n_inv, k + 1)
                run(ln_rstd[:], ln_inv[:].unsqueeze(2).to_broadcast([P, TILES, P]), ACT.Sqrt).then_inc(n_rstd, 1)

            def attention(b):
                need(act, a_kqv, b + 1)
                run(squares[:, 0, :], p4[:, 0, :], ACT.Copy).then_inc(a_k, 1)
                run(squares[:, 2, :], p4[:, 2, :], ACT.Copy).then_inc(a_v, 1)
                need(act, a_ak, b + 1)
                run(squares[:, 3, :], p4[:, 3, :], ACT.Copy).then_inc(a_aks, 1)
                need(act, a_max, b + 1)
                for i in range(TILES):
                    last = run(q_terms[:, i, :], p4[:, i, :], ACT.Exp, bias=row_max[:, i:i + 1])
                last.then_inc(a_exp, 1)
                need(act, a_tr, b + 1)
                run(k_terms[:, 0:2, :], p4[:, 0:2, :], ACT.Copy).then_inc(a_trs, 1)

            def shift_in(n, n_ready):
                need(act, z_done, n_ready + 1)
                run(xs[0:D // 2, :], batch(Z, n)[0:D // 2, :], ACT.Copy)
                run(xs[D // 2:D, 1:S], batch(Z, n)[D // 2:D, 0:S - 1], ACT.Copy).then_inc(xs_ready, 1)

            def body(n, prev, cur):
                for g in range(GROUPS):
                    u = 4 * n + g
                    g3 = (g - 3) % GROUPS

                    def save_values(pair):
                        need(act, valued, 2 * (u - 3) + pair + 1)
                        run(heads_out[:, 2 * g3 + pair, :], pO[:], ACT.Copy).then_inc(o_saved, 1)

                    def place():
                        need(act, transposed, u - 1)
                        need(act, valued, 2 * (u - 2))
                        for q in range(WPT):
                            rows = slice(WIN * q, WIN * (q + 1))
                            run(band[rows, :, :, WIN * q:WIN * (q + 1)], probs_t[rows, :, :, 1, :], ACT.Copy)
                        for q in range(1, WPT):
                            rows = slice(WIN * q, WIN * (q + 1))
                            run(band[WIN * (q - 1):WIN * q, :, :, WIN * q:WIN * (q + 1)],
                                probs_t[rows, :, :, 0, :], ACT.Copy)
                        run(band[P - WIN:P, 0:TILES - 1, :, P:SPAN], probs_t[0:WIN, 1:TILES, :, 0, :], ACT.Copy)\
                            .then_inc(placed, 1)

                    if cur:
                        need(act, k_proj, u + 1)
                        need(act, paired, 2 * u - 1)
                        run(squares[:, 0:2, :], pk, ACT.Square).then_inc(squared, 1)
                        need(act, q_proj, u + 1)
                        need(act, paired, 2 * u)
                        run(squares[:, 2:4, :], pq, ACT.Square).then_inc(squared, 1)
                    if g == 3 and cur:
                        need(act, v_proj, 2 * TILES * (n + 1))
                        shift_in(n + 1, n - 1)
                    if has(g, 3, prev, cur):
                        if g == 3:
                            need(act, o_proj, n)
                        save_values(0)
                    if has(g, 2, prev, cur):
                        need(act, scaled, u - 1)
                        run(probs[:], probs[:], ACT.Exp, scale=QK_SCALE).then_inc(expd, 1)
                    if has(g, 3, prev, cur):
                        save_values(1)
                    if g == 3 and prev:
                        need(act, var_inverted, n)
                        run(ln_rstd[:], ln_inv[:].unsqueeze(2).to_broadcast([P, TILES, P]), ACT.Sqrt)\
                            .then_inc(rstd_set, 1)
                    if cur:
                        need(act, inverted, u + 1)
                        need(act, scaled, u - 1)
                        need(act, spread_k, u)
                        run(inv_k[:], inv2[:, TILES * GH:].unsqueeze(2).to_broadcast([P, TILES * GH, HALF]), ACT.Sqrt)
                        run(inv_q[:, g % 2, :], inv2[:, 0:TILES * GH], ACT.Sqrt).then_inc(rooted, 1)
                    if has(g, 2, prev, cur) and g < 3:
                        place()
                    if g == 2 and cur:
                        need(act, valued, 8 * n)
                        for c in range(2 * TILES):
                            j, half = divmod(c, 2)
                            need(act, v_proj, 2 * TILES * n + c + 1)
                            run(V[:, j, S * half:S * (half + 1)], (pM if c % 2 == 0 else pO)[:], ACT.Copy)\
                                .then_inc(v_saved, 1)
                    if g == 2 and prev:
                        need(act, centred_set, n)
                        run(ln_sq[:], centred[:], ACT.Square).then_inc(ln_squared, 1)
                    if g == 3 and prev:
                        need(act, ln_scaled, n)
                        need(act, z_done, n)
                        run(ln_aff[:], ln_out[:], ACT.Identity, bias=vff[:, 1:2]).then_inc(ln_done, 1)
                        for c, bank in enumerate((pq[:, 0, :], pq[:, 1, :], pk[:, 0, :])):
                            m = CHUNKS[c][1]
                            need(act, gates_up, NC * (n - 1) + c + 1)
                            run(gate[0:m, c, :], bank[0:m, :], ACT.Gelu, bias=vff[0:m, 3 + NC + c:4 + NC + c])\
                                .then_inc(gelu_done, 1)
                    if has(g, 2, prev, cur) and g == 3:
                        place()

            with act.Fori(0, B) as b:
                layer_norm(b)
            act.wait_ge(n_done, B + 1)
            shift_in(0, 0)
            emit(body, act, 0)
            with act.Fori(0, B) as b:
                layer_norm(B + b)
            with act.Fori(0, B) as b:
                attention(b)
            with act.Fori(0, B) as b:
                layer_norm(2 * B + b)
            act.wait_ge(n_done, 3 * B + 1)
            shift_in(ITERS, ITERS)
            emit(body, act, ITERS)

        @block.vector
        def _(dve):
            v = nc.vector
            v.memset(khat[:], 0.0).then_inc(cleared, 1)
            v.memset(band[:], 0.0).then_inc(cleared, 1)
            v.memset(xs[:], 0.0).then_inc(cleared, 1)
            v.memset(z_shift[:], 0.0).then_inc(cleared, 1)
            v.memset(mean_w[:], 1.0 / D).then_inc(cleared, 1)
            for i, primed in enumerate((z_done, n_done, a_done)):
                v.memset(primer[:, i:i + 1], 0.0).then_inc(primed, 1)
            dve.wait_ge(consts_in, CONSTS)
            v.tensor_copy(identity16[:], identity[:]).then_inc(consts_cast, 1)
            v.tensor_copy(mask16[:], squares[:, 0:2, :]).then_inc(consts_cast, 1)
            dve.wait_ge(cleared, 5)

            def layer_norm(k, src, dst):
                need(dve, n_mean, k + 1)
                need(dve, n_done, k + 1)
                v.tensor_tensor(centred[:], src, pM[:], ALU.subtract).then_inc(n_centred, 1)
                need(dve, n_var, k + 1)
                v.tensor_scalar(ln_var[:], pM[:, 0:TILES], LN_EPS, None, ALU.add).then_inc(n_eps, 1)
                need(dve, n_eps, k + 1)
                v.reciprocal(ln_inv[:], ln_var[:]).then_inc(n_inv, 1)
                need(dve, n_spread, k + 1)
                v.tensor_tensor(dst, centred[:], pM[:], ALU.mult).then_inc(n_done, 1)

            def attention(b):
                need(dve, a_kqv, b + 1)
                v.tensor_copy(squares[:, 1, :], p4[:, 1, :]).then_inc(a_q, 1)
                need(dve, a_u, b + 1)
                v.tensor_copy(sumsq[:, 0, :], pO[:]).then_inc(a_us, 1)
                need(dve, a_scores, b + 1)
                v.tensor_reduce(row_max[:, 0:TILES], p4[:], AX_X, ALU.max, negate=True).then_inc(a_max, 1)
                need(dve, a_exp, b + 1)
                v.reduce_sum(row_sum[:, 0:TILES], q_terms[:], AX_X).then_inc(a_sum, 1)
                need(dve, a_sum, b + 1)
                v.reciprocal(inv_sum[:, 0:TILES], row_sum[:, 0:TILES]).then_inc(a_isum, 1)
                need(dve, a_isum, b + 1)
                v.tensor_tensor(q_terms[:], q_terms[:], inv_sum[:, 0:TILES].unsqueeze(2).to_broadcast([P, TILES, S]),
                                ALU.mult).then_inc(a_norm, 1)
                need(dve, a_tr, b + 1)
                v.tensor_copy(k_terms[:, 2:4, :], p4[:, 2:4, :]).then_inc(a_trd, 1)
                need(dve, a_out, b + 1)
                v.tensor_tensor(batch(X, b), batch(X, b), pS[:, 0, :], ALU.add).then_inc(a_done, 1)

            def body(n, prev, cur, st):
                if cur:
                    need(dve, k_prod, 4 * n)
                    layer = n // B - LAYERS * st
                    v.tensor_copy(vqk[:], vecs[:, bass.ds(layer, 1), 0:4].rearrange("p a c -> p (a c)"))\
                        .then_inc(vqk_set, 1)
                    need(dve, vqk_set, n + 1)
                for g in range(GROUPS):
                    u = 4 * n + g

                    def terms(dst, src, vcol, cos, sin):
                        for i, (half, table) in enumerate(((0, cos), (1, sin), (1, cos), (0, sin))):
                            last = v.scalar_tensor_tensor(out=dst[:, i, :], in0=src[:, half, :],
                                                          scalar=vqk[:, vcol + half:vcol + half + 1], in1=table,
                                                          op0=ALU.mult, op1=ALU.mult)
                        return last

                    if cur:
                        need(dve, squared, 2 * u + 1)
                        need(dve, k_rot, u)
                        terms(k_terms, pk, 2, ck, sk).then_inc(k_prod, 1)
                    if has(g, 2, prev, cur):
                        need(dve, expd, u - 1)
                        v.reduce_sum(row_sum[:], probs[:], AX_X).then_inc(rows_summed, 1)
                        need(dve, rows_summed, u - 1)
                        v.reciprocal(inv_sum[:], row_sum[:]).then_inc(sums_inverted, 1)
                    if g == 3 and prev:
                        need(dve, var_done, n)
                        v.tensor_scalar(ln_var[:], pM[:, 0:TILES], LN_EPS, None, ALU.add).then_inc(var_eps, 1)
                        need(dve, var_eps, n)
                        v.reciprocal(ln_inv[:], ln_var[:]).then_inc(var_inverted, 1)
                    if cur:
                        need(dve, summed, u + 1)
                        need(dve, clamped, u)
                        v.transpose(tok_sums[:].rearrange("p a b -> p (a b)"), pM[:, 0:2 * P]).then_inc(by_token, 1)
                        need(dve, by_token, u + 1)
                        need(dve, inverted, u)
                        v.tensor_scalar(norm2[:].rearrange("p (a h) -> p a h", h=GH), tok_sums[:, :, 0:GH],
                                        NORM_EPS ** 2, None, ALU.max).then_inc(clamped, 1)
                        need(dve, clamped, u + 1)
                        need(dve, rooted, u)
                        v.reciprocal(inv2[:], norm2[:]).then_inc(inverted, 1)
                        need(dve, squared, 2 * u + 2)
                        need(dve, q_rot, u)
                        terms(q_terms, pq, 0, cq, sq_).then_inc(q_prod, 1)
                    if has(g, 2, prev, cur):
                        need(dve, normed, u - 1)
                        need(dve, placed, u - 2)
                        v.transpose(probs_t[:].rearrange("p j h b t -> p (j h b t)"),
                                    probs[:].rearrange("p r s -> p (r s)")).then_inc(transposed, 1)
                    if g == 3 and prev:
                        need(dve, rstd_spread, n)
                        v.scalar_tensor_tensor(out=ln_out[:], in0=centred[:], scalar=vff[:, 0:1], in1=pM[:],
                                               op0=ALU.mult, op1=ALU.mult).then_inc(ln_scaled, 1)
                    if has(g, 1, prev, cur):
                        need(dve, scored, u)
                        scores = pS[:].rearrange("p b (r s) -> p (b r) s", s=2 * WIN)
                        v.reduce_max(row_max[:], scores, AX_X).then_inc(maxed, 1)
                        need(dve, maxed, u)
                        need(dve, transposed, u - 1)
                        v.tensor_tensor(probs[:], scores, row_max[:].unsqueeze(2).to_broadcast([P, TILES * GH, 2 * WIN]),
                                        ALU.subtract).then_inc(shifted, 1)
                    if cur:
                        need(dve, spread_k, u + 1)
                        need(dve, k_rot, u + 1)
                        need(dve, khat_in, 16 * GH * u)
                        v.tensor_tensor(k_normed[:], k_rotated[:], pM[:].unsqueeze(1).to_broadcast([P, 2, S]),
                                        ALU.mult).then_inc(k_norm, 1)
                    if g == 2 and prev:
                        need(dve, z_done, n)
                        layer = (n - 1) // B - LAYERS * st
                        v.tensor_copy(vff[:], vecs[:, bass.ds(layer, 1), 4:].rearrange("p a c -> p (a c)"))\
                            .then_inc(vff_set, 1)
                        need(dve, o_proj, n)
                        v.tensor_tensor(z_mid[:], batch(Z, n - 1), pO[:], ALU.add).then_inc(z_mid_set, 1)
                        need(dve, z_mid_set, n)
                        v.tensor_copy(z_shift[0:D // 2, :], z_mid[0:D // 2, :])
                        v.tensor_copy(z_shift[D // 2:D, 1:S], z_mid[D // 2:D, 0:S - 1]).then_inc(z_shifted, 1)
                        need(dve, z_shifted, n)
                        need(dve, mean_done, n)
                        v.tensor_tensor(centred[:], z_shift[:], pM[:], ALU.subtract).then_inc(centred_set, 1)
                    if g == 3 and prev:
                        need(dve, vff_set, n)
                        for c, bank in enumerate((pk[:, 1, :], pM[:], pO[:])):
                            m = CHUNKS[c][1]
                            need(dve, gelu_done, NC * (n - 1) + c + 1)
                            need(dve, values_up, NC * (n - 1) + c + 1)
                            v.scalar_tensor_tensor(out=hidden[0:m, c, :], in0=bank[0:m, :], scalar=vff[0:m, 3 + c:4 + c],
                                                   in1=gate[0:m, c, :], op0=ALU.add, op1=ALU.mult)\
                                .then_inc(hidden_set, 1)
                        need(dve, ff_down, n)
                        v.scalar_tensor_tensor(out=batch(Z, n - 1), in0=pM[:], scalar=vff[:, 2:3], in1=z_mid[:],
                                               op0=ALU.add, op1=ALU.add).then_inc(z_done, 1)

            with dve.Fori(0, B) as b:
                layer_norm(b, batch(X, b), batch(Z, b))
            dve.wait_ge(n_done, B + 1)
            emit(lambda n, prev, cur: body(n, prev, cur, 0), dve, 0)
            dve.wait_ge(z_done, ITERS + 1)
            v.scalar_tensor_tensor(out=X[:], in0=Z[:], scalar=0.5, in1=X[:], op0=ALU.mult, op1=ALU.add)\
                .then_inc(x_updated, 1)
            dve.wait_ge(x_updated, 1)
            with dve.Fori(0, B) as b:
                layer_norm(B + b, batch(X, b), batch(Z, b))
            with dve.Fori(0, B) as b:
                attention(b)
            dve.wait_ge(a_done, B + 1)
            with dve.Fori(0, B) as b:
                layer_norm(2 * B + b, batch(X, b), batch(Z, b))
            dve.wait_ge(n_done, 3 * B + 1)
            emit(lambda n, prev, cur: body(n, prev, cur, 1), dve, ITERS)
            dve.wait_ge(z_done, 2 * ITERS + 1)
            v.scalar_tensor_tensor(out=X[:], in0=Z[:], scalar=0.5, in1=X[:], op0=ALU.mult, op1=ALU.add)\
                .then_inc(x_updated, 1)

        @block.gpsimd
        def _(pool):
            tt = nc.gpsimd.tensor_tensor

            def body(n, prev, cur):
                for g in range(GROUPS):
                    u = 4 * n + g
                    if has(g, 2, prev, cur):
                        need(pool, shifted, u - 1)
                        need(pool, rooted, u - 1)
                        tt(probs[:], probs[:], inv_q[:, g % 2, :].unsqueeze(2).to_broadcast([P, TILES * GH, 2 * WIN]),
                           ALU.mult).then_inc(scaled, 1)
                    if cur:
                        for i, qk in enumerate((1, 0)):
                            need(pool, squared, 2 * u + i + 1)
                            need(pool, summed, u)
                            tt(sumsq[:, qk, :], squares[:, 2 * i, :], squares[:, 2 * i + 1, :], ALU.add)\
                                .then_inc(paired, 1)
                        need(pool, k_prod, u + 1)
                        need(pool, k_norm, u)
                        tt(k_rotated[:, 0, :], k_terms[:, 0, :], k_terms[:, 1, :], ALU.subtract)
                        tt(k_rotated[:, 1, :], k_terms[:, 2, :], k_terms[:, 3, :], ALU.add).then_inc(k_rot, 1)
                    if has(g, 2, prev, cur):
                        need(pool, sums_inverted, u - 1)
                        tt(probs[:], probs[:], inv_sum[:].unsqueeze(2).to_broadcast([P, TILES * GH, 2 * WIN]), ALU.mult)\
                            .then_inc(normed, 1)
                    if cur:
                        need(pool, q_prod, u + 1)
                        need(pool, scored, u - 1)
                        qr = q_rotated[:, g % 2, :, :]
                        tt(qr[:, 0, :], q_terms[:, 0, :], q_terms[:, 1, :], ALU.subtract)
                        tt(qr[:, 1, :], q_terms[:, 2, :], q_terms[:, 3, :], ALU.add).then_inc(q_rot, 1)

            emit(body, pool, 0)
            pool.wait_ge(a_done, B + 1)
            emit(body, pool, ITERS)


def kernel(**inputs):
    import numpy as np
    import concourse.bacc as bacc
    from concourse.bass_utils import run_bass_kernel_spmd

    a = {k: np.asarray(x) for k, x in inputs.items()}
    f = lambda name: a["L0_ffn_" + name]
    w = f("Wqkv").reshape(LAYERS, D, 3, GROUPS, GH, 2, HALF)
    vec = np.zeros((P, LAYERS, VEC), np.float32)
    for c, name in ((0, "q_scale"), (2, "k_scale")):
        halves = f(name).reshape(LAYERS, 2, HALF).transpose(2, 0, 1)
        vec[:, :, c:c + 2] = np.tile(halves, (GH, 1, 1))
    vec[:, :, 4], vec[:, :, 5], vec[:, :, 6] = f("ln_g").T, f("ln_b").T, f("b2").T
    b1 = f("b1")
    w2 = np.zeros((LAYERS, P, NC, D), np.float32)
    for c, (at, m) in enumerate(CHUNKS):
        vec[0:m, :, 7 + c] = b1[:, at:at + m].T
        vec[0:m, :, 7 + NC + c] = b1[:, FF + at:FF + at + m].T
        w2[:, 0:m, c] = f("W2")[:, at:at + m]

    half = np.arange(0, DH, 2, dtype=np.float32)
    inv_freq = (1.0 / np.float32(10000.0) ** (half / np.float32(DH))).astype(np.float32)
    t = np.arange(S, dtype=np.float32)
    angle = (inv_freq[:, None] * t[None, :]).astype(np.float32)
    base = ((half + np.float32(0.4 * DH)) / np.float32(1.4 * DH)).astype(np.float32)
    scale = (base[:, None] ** ((t - S // 2) / (WIN // 2))[None, :]).astype(np.float32)
    cos, sin = np.cos(angle), np.sin(angle)
    rot = np.stack([cos * scale, sin * scale, cos * (1 / scale), sin * (1 / scale)], 1).astype(np.float32)
    rot = np.tile(rot, (GH, 1, 1))
    r, s = np.arange(P)[:, None] % WIN, np.arange(2 * WIN)[None, :]
    allowed = (s >= r) & (s <= r + WIN)
    mask = np.where(allowed, 0.0, MASKED).astype(np.float32)[:, None, None, :]
    mask = np.broadcast_to(mask, (P, TILES, GH, 2 * WIN)).copy()
    mask[0:WIN, 0, :, 0:WIN] = MASKED
    sel = (np.arange(P)[:, None] // HALF == np.arange(WIN)[None, :]).astype(np.float32)

    arrays = {
        "x_t": a["L0_attn_x"].transpose(2, 0, 1),
        "w_qk": w[:, :, 0:2].transpose(0, 3, 1, 2, 5, 4, 6).reshape(LAYERS, GROUPS, D, 4 * P),
        "w_v": f("Wqkv")[:, :, 2 * HEADS * DH:],
        "w_o": f("Wo").reshape(LAYERS, PAIRS, P, D).transpose(0, 2, 1, 3).reshape(LAYERS, P, PAIRS * D),
        "w_1": f("W1"),
        "w_2": w2.reshape(LAYERS, P, NC * D),
        "vec": vec,
        "rot": rot,
        "mask": mask.reshape(P, 2, S),
        "ident": np.eye(P, dtype=np.float32),
        "a_w": np.concatenate([a["L0_attn_W" + c].T for c in "kqvab"], 1),
        "sel": sel,
    }
    arrays = {k: np.ascontiguousarray(x) for k, x in arrays.items()}
    nc = bacc.Bacc("TRN2", target_bir_lowering=False, num_devices=1)
    args = {k: nc.dram_tensor(k + "_dram", x.shape, F32, kind="ExternalInput").ap() for k, x in arrays.items()}
    out = nc.dram_tensor("out_dram", (P, B, S), F32, kind="ExternalOutput").ap()
    macaron(nc, **args, out=out)
    r = run_bass_kernel_spmd(nc, [{k + "_dram": x for k, x in arrays.items()}], core_ids=[0])
    return np.ascontiguousarray(r.results[0]["out_dram"].transpose(1, 2, 0))
```

```python
from contextlib import ExitStack

import concourse.bass as bass
from concourse import mybir

F32 = mybir.dt.float32
F32R = mybir.dt.float32r
BF16 = mybir.dt.bfloat16
ALU = mybir.AluOpType
ACT = mybir.ActivationFunctionType
AX_X = mybir.AxisListType.X

P = 128
B, S, D = 4, 512, 128
LAYERS, HEADS, DH, WIN = 6, 16, 64, 32
HALF = DH // 2
GH = P // HALF
GROUPS = HEADS // GH
TILES = S // P
WPT = P // WIN
PAIRS = HEADS // 2
V_COLS = GH * DH
V_CHUNKS = (2, 2, 4, 0)
FF = D * 4 * 2 // 3
CHUNKS = [(c, min(P, FF - c)) for c in range(0, FF, P)]
NC = len(CHUNKS)
ITERS = LAYERS * B
SPAN = P + WIN
QK_SCALE = 8.0
LN_EPS = 1e-5
NORM_EPS = 1e-12
MASKED = -1e30
VEC = 6 + 2 * NC + 1


def need(eng, sem, count):
    if not isinstance(count, int) or count > 0:
        eng.wait_ge(sem, count)


def macaron(nc, x_t, w_qk, w_v, w_o, w_1, w_2, vec, rot, mask, ident, a_w, sel, spread_sel, out):
    with ExitStack() as ctx:
        def sb(name, shape, dt=F32):
            return ctx.enter_context(nc.sbuf_tensor(name, shape, dt))

        def ps(name, shape):
            return ctx.enter_context(nc.psum_tensor(name, shape, F32))

        def sem(name):
            return ctx.enter_context(nc.semaphore(name))

        X = sb("X", [P, B, S])
        Z = sb("Z", [P, B, S])
        wqk = sb("wqk", [P, GROUPS, 4, P])
        wv = sb("wv", [P, HEADS * DH])
        wo = sb("wo", [P, PAIRS, D])
        w1 = sb("w1", [P, 2 * FF])
        w2 = sb("w2", [P, NC, D])
        attn_w = sb("attn_w", [P, 5, D])
        vecs = sb("vecs", [P, LAYERS, VEC])
        vqk = sb("vqk", [P, 4])
        vff = sb("vff", [P, VEC - 4])
        rotary = sb("rotary", [P, 4, S])
        cq, sq_, ck, sk = (rotary[:, i, :] for i in range(4))
        identity = sb("identity", [P, P])
        identity16 = sb("identity16", [P, P], BF16)
        mask16 = sb("mask16", [P, 2, 2 * GH * 2 * WIN], BF16)
        head_sel = sb("head_sel", [P, WIN])
        mean_w = sb("mean_w", [P, P])
        xs = sb("xs", [P, S])
        squares = sb("squares", [P, 4, S])
        sumsq = sb("sumsq", [P, 2, S])
        q_terms = sb("q_terms", [P, 4, S])
        k_terms = sb("k_terms", [P, 4, S])
        q_rotated = sb("q_rotated", [P, 2, 2, S])
        k_rotated = sb("k_rotated", [P, 2, S])
        k_normed = sb("k_normed", [P, 2, S])
        khat = sb("khat", [P, 2, GH, WIN + S])
        tok_sums = sb("tok_sums", [P, 2 * TILES, WIN])
        norm2 = sb("norm2", [P, 2 * TILES * GH])
        inv2 = sb("inv2", [P, 2 * TILES * GH])
        inv_q = sb("inv_q", [P, 2, TILES * GH])
        inv_k = sb("inv_k", [P, TILES, GH])
        k_split = sb("k_split", [P, TILES, WIN], F32R)
        turned = sb("turned", [P, TILES * WIN])
        k_rows = sb("k_rows", [P, TILES * WIN], F32R)
        ln_split = sb("ln_split", [P, TILES, WIN], F32R)
        ln_rows = sb("ln_rows", [P, TILES * WIN], F32R)
        row_sel = sb("row_sel", [P, WPT, P], F32R)
        row_max = sb("row_max", [P, TILES * GH])
        row_sum = sb("row_sum", [P, TILES * GH])
        inv_sum = sb("inv_sum", [P, TILES * GH])
        probs = sb("probs", [P, TILES * GH, 2 * WIN])
        probs_t = sb("probs_t", [P, TILES, GH, 2, WIN])
        band = sb("band", [P, TILES, GH, SPAN])
        V = sb("V", [P, TILES, HEADS * DH])
        heads_out = sb("heads_out", [P, PAIRS, S])
        z_mid = sb("z_mid", [P, S])
        z_shift = sb("z_shift", [P, S])
        centred = sb("centred", [P, S])
        ln_sq = sb("ln_sq", [P, S])
        ln_var = sb("ln_var", [P, TILES])
        ln_inv = sb("ln_inv", [P, TILES])
        ln_rstd = sb("ln_rstd", [P, TILES])
        ln_out = sb("ln_out", [P, S])
        ln_aff = sb("ln_aff", [P, S])
        gate = sb("gate", [P, NC, S])
        hidden = sb("hidden", [P, NC, S])

        primer = sb("primer", [P, 3])

        p4 = ps("p4", [P, 4, S])
        pq, pk = p4[:, 0:2, :], p4[:, 2:4, :]
        pS = ps("pS", [P, 2, S])
        pO = ps("pO", [P, S])
        pM = ps("pM", [P, S])

        V_BANK = (pO, pM, pO, pM)
        O_BANK = ((pO, pM), (pO, pM), (pM, pO), (pM, pO))
        K_BANK = (pO, pO, pO, pM)

        consts_in, consts_cast, cleared = sem("consts_in"), sem("consts_cast"), sem("cleared")
        wqk_in = [sem(f"wqk_in{g}") for g in range(GROUPS)]
        wv_in, wo_in, wff_in = sem("wv_in"), sem("wo_in"), sem("wff_in")
        xs_ready = sem("xs_ready")
        q_proj, k_proj, squared, paired = sem("q_proj"), sem("k_proj"), sem("squared"), sem("paired")
        q_prod, k_prod, q_rot, k_rot = sem("q_prod"), sem("k_prod"), sem("q_rot"), sem("k_rot")
        summed, by_token, clamped, inverted, rooted = (
            sem("summed"), sem("by_token"), sem("clamped"), sem("inverted"), sem("rooted"))
        k_low, k_rowed, rstd_low, rstd_rowed = sem("k_low"), sem("k_rowed"), sem("rstd_low"), sem("rstd_rowed")
        k_turned, rstd_turned, n_turned = sem("k_turned"), sem("rstd_turned"), sem("n_turned")
        spread_k, k_norm, khat_in = sem("spread_k"), sem("k_norm"), sem("khat_in")
        scored, maxed, shifted, scaled, expd = (sem("scored"), sem("maxed"), sem("shifted"), sem("scaled"), sem("expd"))
        rows_summed, sums_inverted, normed = sem("rows_summed"), sem("sums_inverted"), sem("normed")
        transposed, placed, valued, o_saved = sem("transposed"), sem("placed"), sem("valued"), sem("o_saved")
        v_proj, v_saved = sem("v_proj"), sem("v_saved")
        vqk_set, vff_set = sem("vqk_set"), sem("vff_set")
        o_proj, z_mid_set, z_shifted = sem("o_proj"), sem("z_mid_set"), sem("z_shifted")
        mean_done, centred_set, ln_squared, var_done = (sem("mean_done"), sem("centred_set"), sem("ln_squared"), sem("var_done"))
        var_eps, var_inverted, rstd_set, rstd_spread = (sem("var_eps"), sem("var_inverted"), sem("rstd_set"), sem("rstd_spread"))
        ln_scaled, ln_done = sem("ln_scaled"), sem("ln_done")
        gates_up, values_up, gelu_done, hidden_set = (sem("gates_up"), sem("values_up"), sem("gelu_done"), sem("hidden_set"))
        ff_down, z_done = sem("ff_down"), sem("z_done")
        n_mean, n_centred, n_squared, n_var, n_eps, n_inv, n_rstd, n_low, n_rowed, n_spread, n_done = (
            sem("n_" + s) for s in ("mean", "centred", "squared", "var", "eps", "inv", "rstd", "low", "rowed", "spread", "done"))
        x_updated = sem("x_updated")
        a_kqv, a_k, a_v, a_q, a_ak, a_u, a_aks, a_us, a_scores, a_max, a_exp = (
            sem("a_" + s) for s in ("kqv", "k", "v", "q", "ak", "u", "aks", "us", "scores", "max", "exp"))
        a_sum, a_isum, a_norm, a_tr, a_trs, a_trd, a_out, a_done = (
            sem("a_" + s) for s in ("sum", "isum", "norm", "tr", "trs", "trd", "out", "done"))
        out_stored = sem("out_stored")

        block = ctx.enter_context(nc.Block())
        CONSTS = 8 * 16

        def has(g, back, prev, cur):
            return cur if g >= back else prev

        def batch(t, n):
            return t[:, bass.ds(n % B, 1), :].rearrange("p a s -> p (a s)")

        def emit(body, eng, n0):
            body(n0, prev=False, cur=True)
            with eng.Fori(n0 + 1, n0 + ITERS) as n:
                body(n, prev=True, cur=True)
            body(n0 + ITERS, prev=True, cur=False)

        @block.sync
        def _(sp):
            for dst, src in ((X[:], x_t), (vecs[:], vec), (rotary[:], rot), (identity[:], ident),
                             (squares[:, 0:2, :], mask), (head_sel[:], sel), (squares[:, 2, :], spread_sel),
                             (attn_w[:].rearrange("p a m -> p (a m)"), a_w)):
                sp.dma_start(dst, src).then_inc(consts_in, 16)

            def load_qk(layer, g):
                sp.dma_start(wqk[:, g, :, :].rearrange("p a m -> p (a m)"),
                             w_qk[bass.ds(layer, 1), g, :, :].rearrange("a p m -> p (a m)")).then_inc(wqk_in[g], 16)

            def load_v(layer):
                sp.dma_start(wv[:], w_v[bass.ds(layer, 1), :, :].rearrange("a p m -> p (a m)")).then_inc(wv_in, 16)

            def load_o(layer):
                sp.dma_start(wo[:].rearrange("p a m -> p (a m)"),
                             w_o[bass.ds(layer, 1), :, :].rearrange("a p m -> p (a m)")).then_inc(wo_in, 16)

            def load_ff(layer):
                sp.dma_start(w1[:], w_1[bass.ds(layer, 1), :, :].rearrange("a p m -> p (a m)")).then_inc(wff_in, 16)
                sp.dma_start(w2[:].rearrange("p a m -> p (a m)"),
                             w_2[bass.ds(layer, 1), :, :].rearrange("a p m -> p (a m)")).then_inc(wff_in, 16)

            for g in range(GROUPS):
                load_qk(0, g)
            load_v(0)
            load_o(0)
            load_ff(0)
            sp.wait_ge(cleared, 7)

            def spread(u):
                need(sp, k_norm, u + 1)
                for h in range(GH):
                    sp.dma_start(khat[HALF * h:HALF * (h + 1), :, h, WIN:],
                                 k_normed[HALF * h:HALF * (h + 1), :, :]).then_inc(khat_in, 16)

            def layer_loads(lay, first, last):
                for row in range(B):
                    for g in range(GROUPS):
                        spread(4 * (B * lay + row) + g)
                        if row == 0 and g == 3 and not first:
                            load_o(lay % LAYERS)
                        if row == 1 and g == 0 and not first:
                            load_ff(lay % LAYERS)
                        if row == B - 1 and not last:
                            load_qk((lay + 1) % LAYERS, g)
                            if g == 3:
                                load_v((lay + 1) % LAYERS)

            layer_loads(0, True, False)
            with sp.Fori(1, 2 * LAYERS - 1) as lay:
                layer_loads(lay, False, False)
            layer_loads(2 * LAYERS - 1, False, True)
            sp.wait_ge(x_updated, 2)
            sp.dma_start(out, X[:]).then_inc(out_stored, 16)
            sp.wait_ge(out_stored, 16)

        @block.tensor
        def _(pe):
            mm = nc.tensor.matmul
            pe.wait_ge(consts_in, CONSTS)
            pe.wait_ge(consts_cast, 3)
            pe.wait_ge(cleared, 7)

            def spread(rows, bank=pM):
                by_window = bank[:].rearrange("p (j q t) -> p j q t", j=TILES, q=WPT)
                for q in range(WPT):
                    last = mm(by_window[:, :, q, :], row_sel[:, q, :], rows[:], start=True, stop=True)
                return last

            def layer_norm(k, src):
                need(pe, n_done, k + 1)
                mm(pM[:], mean_w[:], src, start=True, stop=True).then_inc(n_mean, 1)
                need(pe, n_squared, k + 1)
                for j in range(TILES):
                    last = mm(pM[:, j:j + 1], ln_sq[:, P * j:P * (j + 1)], mean_w[:, 0:1], start=True, stop=True)
                last.then_inc(n_var, 1)
                need(pe, n_rowed, k + 1)
                spread(ln_rows).then_inc(n_spread, 1)

            def attention(b):
                wk_, wq_, wv_, wa_, wb_ = (attn_w[:, i, :] for i in range(5))
                need(pe, a_done, b + 1)
                mm(p4[:, 0, :], wk_, batch(Z, b), start=True, stop=True)
                mm(p4[:, 1, :], wq_, batch(Z, b), start=True, stop=True)
                mm(p4[:, 2, :], wv_, batch(Z, b), start=True, stop=True).then_inc(a_kqv, 1)
                need(pe, a_k, b + 1)
                mm(p4[:, 3, :], wa_, squares[:, 0, :], start=True, stop=True).then_inc(a_ak, 1)
                need(pe, a_v, b + 1)
                for j in range(TILES):
                    last = mm(pO[:, P * j:P * (j + 1)], squares[:, 2, P * j:P * (j + 1)], wb_, start=True, stop=True)
                last.then_inc(a_u, 1)
                need(pe, a_aks, b + 1)
                need(pe, a_q, b + 1)
                for i in range(TILES):
                    last = mm(p4[:, i, :], squares[:, 1, P * i:P * (i + 1)], squares[:, 3, :], start=True, stop=True)
                last.then_inc(a_scores, 1)
                need(pe, a_norm, b + 1)
                for j in range(TILES):
                    for i in range(TILES):
                        last = mm(p4[:, j, P * i:P * (i + 1)], q_terms[:, i, P * j:P * (j + 1)], identity[:],
                                  start=True, stop=True)
                last.then_inc(a_tr, 1)
                need(pe, a_trs, b + 1)
                need(pe, a_trd, b + 1)
                need(pe, a_us, b + 1)
                for j in range(TILES):
                    last = mm(pS[:, 0, :], sumsq[:, 0, P * j:P * (j + 1)], k_terms[:, j, :],
                              start=(j == 0), stop=(j == TILES - 1))
                last.then_inc(a_out, 1)

            def body(n, prev, cur, st):
                for g in range(GROUPS):
                    u = 4 * n + g

                    def project(bank, w, done):
                        mm(bank[:, 0, :], wqk[:, g, w, :], xs[:], start=True, stop=True)
                        mm(bank[:, 1, :], wqk[:, g, w + 1, :], xs[:], start=True, stop=True).then_inc(done, 1)

                    def project_v(c):
                        heads = V_COLS * (g + c // 2)
                        for jj in range(2):
                            j = 2 * (c % 2) + jj
                            last = mm(V_BANK[c][:, V_COLS * jj:V_COLS * (jj + 1)],
                                      xs[:, P * j:P * (j + 1)], wv[:, heads:heads + V_COLS], start=True, stop=True)
                        last.then_inc(v_proj, 1)

                    def values(pair):
                        bank = O_BANK[g][pair]
                        for hh in range(2):
                            h = 2 * pair + hh
                            feat = (GH * ((g - 3) % GROUPS) + h) * DH
                            for j in range(TILES):
                                wide = min(SPAN, S - P * j)
                                last = mm(bank[DH * hh:DH * (hh + 1), P * j:P * j + wide],
                                          V[:, j, feat:feat + DH], band[:, j, h, 0:wide],
                                          start=(j == 0), stop=(j == TILES - 1), skip_group_check=True)
                        last.then_inc(valued, 1)

                    def scores(half):
                        qr = q_rotated[:, (g - 1) % 2, :, :]
                        mm(pS[:, half, :], identity16[:], mask16[:, half, :], start=True, stop=False,
                           skip_group_check=True)
                        for j in range(2):
                            cols = j * GH * 2 * WIN
                            for ab in range(2):
                                for q in range(WPT):
                                    w = WPT * (2 * half + j) + q
                                    last = mm(pS[WIN * q:WIN * (q + 1), half, cols:cols + GH * 2 * WIN],
                                              qr[:, ab, WIN * w:WIN * (w + 1)],
                                              khat[:, ab, :, WIN * w:WIN * (w + 2)],
                                              start=False, stop=(ab == 1), skip_group_check=True)
                        return last

                    def spread_keys():
                        need(pe, k_rowed, u + 1)
                        need(pe, o_saved, 2 * u - 5)
                        spread(k_rows, K_BANK[g]).then_inc(spread_k, 1)

                    def lengths():
                        need(pe, paired, 2 * u + 2)
                        need(pe, v_saved, 2 * u + 2)
                        for qk in range(2):
                            by_window = sumsq[:, qk, :].rearrange("p (j q t) -> p j q t", j=TILES, q=WPT)
                            for q in range(WPT):
                                last = mm(pM[WIN * q:WIN * (q + 1), P * qk:P * (qk + 1)], head_sel[:],
                                          by_window[:, :, q, :], start=True, stop=True, skip_group_check=True)
                        last.then_inc(summed, 1)

                    if cur:
                        need(pe, xs_ready, n + 1 + st)
                        need(pe, wqk_in[g], 16 * (n // B + 1))
                        need(pe, k_prod, u)
                        project(pk, 2, k_proj)
                    if cur:
                        need(pe, q_prod, u)
                        if g == 0 and prev:
                            need(pe, z_done, n)
                        project(pq, 0, q_proj)
                    if g < 3 and cur:
                        need(pe, wv_in, 16 * (n // B + 1))
                        need(pe, k_norm, u)
                        need(pe, o_saved, 2 * u - 6)
                        project_v(0)
                        project_v(1)
                    if g == 3 and prev:
                        need(pe, ln_squared, n)
                        need(pe, v_saved, 8 * n + 8 if cur else 8 * n)
                        for j in range(TILES):
                            last = mm(pO[:, j:j + 1], ln_sq[:, P * j:P * (j + 1)], mean_w[:, 0:1], start=True, stop=True)
                        last.then_inc(var_done, 1)
                    if has(g, 1, prev, cur):
                        need(pe, shifted, u - 1)
                        need(pe, q_rot, u)
                        need(pe, khat_in, 16 * GH * u)
                        scores(0)
                    if g < 3 and cur:
                        lengths()
                    if has(g, 1, prev, cur):
                        scores(1).then_inc(scored, 1)
                    if g == 3 and cur:
                        lengths()
                    if g == 3 and prev:
                        need(pe, rstd_rowed, n)
                        spread(ln_rows, pO).then_inc(rstd_spread, 1)
                    if has(g, 3, prev, cur):
                        need(pe, placed, u - 2)
                        need(pe, v_saved, 2 * u + 2 if cur else 8 * n)
                        if cur:
                            need(pe, by_token, u + 1)
                        else:
                            need(pe, k_norm, 4 * n)
                        values(0)
                        if g == 3 and prev:
                            need(pe, ln_scaled, n)
                        values(1)
                    if g == 2 and prev:
                        need(pe, wo_in, 16 * ((n - 1) // B + 1))
                        need(pe, o_saved, 8 * n - 1)
                        for i in range(PAIRS // 2):
                            mm(pM[:], wo[:, i, :], heads_out[:, i, :], start=(i == 0), stop=False)
                        need(pe, o_saved, 8 * n)
                    if cur and not (g == 3 and prev):
                        spread_keys()
                    if g == 2 and prev:
                        for i in range(PAIRS // 2, PAIRS):
                            last = mm(pM[:], wo[:, i, :], heads_out[:, i, :], start=False, stop=(i == PAIRS - 1))
                        last.then_inc(o_proj, 1)
                    if g == 2 and cur:
                        need(pe, k_norm, u + 1)
                        project_v(2)
                        if prev:
                            need(pe, z_mid_set, n)
                        project_v(3)
                    if g == 2 and prev:
                        need(pe, z_shifted, n)
                        if cur:
                            need(pe, v_saved, 2 * u + 3)
                        mm(pO[:], mean_w[:], z_shift[:], start=True, stop=True).then_inc(mean_done, 1)
                    if g == 3 and prev:
                        need(pe, ln_done, n)
                        need(pe, wff_in, 32 * ((n - 1) // B + 1))
                        for c, bank in enumerate((pq[:, 0, :], pq[:, 1, :], pk[:, 0, :])):
                            if cur:
                                need(pe, q_prod if c < 2 else k_prod, u + 1)
                            f, m = CHUNKS[c]
                            mm(bank[0:m, :], w1[:, FF + f:FF + f + m], ln_aff[:], start=True, stop=True)\
                                .then_inc(gates_up, 1)
                        if cur:
                            spread_keys()
                        need(pe, o_saved, 2 * (u - 3) + 2 if cur else 8 * n)
                        for c, bank in enumerate((pk[:, 1, :], pO[:], pM[:])):
                            if c == 2 and cur:
                                need(pe, k_norm, u + 1)
                            f, m = CHUNKS[c]
                            mm(bank[0:m, :], w1[:, f:f + m], ln_aff[:], start=True, stop=True).then_inc(values_up, 1)
                        for c in range(NC):
                            need(pe, hidden_set, NC * (n - 1) + c + 1)
                            m = CHUNKS[c][1]
                            last = mm(pq[:, 0, :], w2[0:m, c, :], hidden[0:m, c, :], start=(c == 0), stop=(c == NC - 1))
                        last.then_inc(ff_down, 1)

            with pe.Fori(0, B) as b:
                layer_norm(b, batch(X, b))
            emit(lambda n, prev, cur: body(n, prev, cur, 0), pe, 0)
            pe.wait_ge(x_updated, 1)
            with pe.Fori(0, B) as b:
                layer_norm(B + b, batch(X, b))
            pe.wait_ge(n_done, 2 * B + 1)
            with pe.Fori(0, B) as b:
                attention(b)
            pe.wait_ge(a_done, B + 1)
            with pe.Fori(0, B) as b:
                layer_norm(2 * B + b, batch(X, b))
            emit(lambda n, prev, cur: body(n, prev, cur, 1), pe, ITERS)

        @block.scalar
        def _(act):
            run = nc.scalar.activation
            act.wait_ge(cleared, 7)

            def root_rstd():
                run(ln_split[:, :, 0:GH], ln_inv[:].unsqueeze(2).to_broadcast([P, TILES, GH]), ACT.Sqrt)
                return run(ln_rstd[:], ln_inv[:], ACT.Sqrt)

            def layer_norm(k):
                need(act, n_centred, k + 1)
                run(ln_sq[:], centred[:], ACT.Square).then_inc(n_squared, 1)
                need(act, n_inv, k + 1)
                root_rstd().then_inc(n_rstd, 1)

            def attention(b):
                need(act, a_kqv, b + 1)
                run(squares[:, 0, :], p4[:, 0, :], ACT.Copy).then_inc(a_k, 1)
                run(squares[:, 2, :], p4[:, 2, :], ACT.Copy).then_inc(a_v, 1)
                need(act, a_ak, b + 1)
                run(squares[:, 3, :], p4[:, 3, :], ACT.Copy).then_inc(a_aks, 1)
                need(act, a_max, b + 1)
                for i in range(TILES):
                    last = run(q_terms[:, i, :], p4[:, i, :], ACT.Exp, bias=row_max[:, i:i + 1])
                last.then_inc(a_exp, 1)
                need(act, a_tr, b + 1)
                run(k_terms[:, 0:2, :], p4[:, 0:2, :], ACT.Copy).then_inc(a_trs, 1)

            def shift_in(n, n_ready):
                need(act, z_done, n_ready + 1)
                run(xs[0:D // 2, :], batch(Z, n)[0:D // 2, :], ACT.Copy)
                run(xs[D // 2:D, 1:S], batch(Z, n)[D // 2:D, 0:S - 1], ACT.Copy).then_inc(xs_ready, 1)

            def body(n, prev, cur):
                for g in range(GROUPS):
                    u = 4 * n + g
                    g3 = (g - 3) % GROUPS

                    def save_values(pair):
                        need(act, valued, 2 * (u - 3) + pair + 1)
                        run(heads_out[:, 2 * g3 + pair, :], O_BANK[g][pair][:], ACT.Copy).then_inc(o_saved, 1)

                    def save_v(c):
                        j, heads = 2 * (c % 2), V_COLS * (g + c // 2)
                        need(act, v_proj, 2 * u + c + 1)
                        run(V[:, j:j + 2, heads:heads + V_COLS], V_BANK[c][:].rearrange("p (j f) -> p j f", j=2),
                            ACT.Copy).then_inc(v_saved, 1)

                    def place(unit):
                        need(act, transposed, unit + 1)
                        need(act, valued, 2 * unit)
                        for q in range(WPT):
                            rows = slice(WIN * q, WIN * (q + 1))
                            run(band[rows, :, :, WIN * q:WIN * (q + 1)], probs_t[rows, :, :, 1, :], ACT.Copy)
                        for q in range(1, WPT):
                            rows = slice(WIN * q, WIN * (q + 1))
                            run(band[WIN * (q - 1):WIN * q, :, :, WIN * q:WIN * (q + 1)],
                                probs_t[rows, :, :, 0, :], ACT.Copy)
                        run(band[P - WIN:P, 0:TILES - 1, :, P:SPAN], probs_t[0:WIN, 1:TILES, :, 0, :], ACT.Copy)\
                            .then_inc(placed, 1)

                    if cur:
                        need(act, k_proj, u + 1)
                        need(act, paired, 2 * u - 1)
                        run(squares[:, 0:2, :], pk, ACT.Square).then_inc(squared, 1)
                    if cur:
                        need(act, q_proj, u + 1)
                        need(act, paired, 2 * u)
                        run(squares[:, 2:4, :], pq, ACT.Square).then_inc(squared, 1)
                    if has(g, 2, prev, cur):
                        need(act, scaled, u - 1)
                        run(probs[:], probs[:], ACT.Exp, scale=QK_SCALE).then_inc(expd, 1)
                    if g < 3 and cur:
                        need(act, valued, 2 * u - 6)
                        save_v(0)
                        save_v(1)
                    if g == 3 and prev:
                        need(act, var_inverted, n)
                        root_rstd().then_inc(rstd_set, 1)
                    if g in (1, 2) and has(g, 3, prev, cur):
                        place(u - 3)
                    if cur:
                        need(act, inverted, u + 1)
                        need(act, scaled, u - 1)
                        need(act, k_rowed, u)
                        keys = inv2[:, TILES * GH:].rearrange("p (j h) -> p j h", h=GH)
                        run(k_split[:, :, 0:GH], keys, ACT.Sqrt)
                        run(inv_k[:], keys, ACT.Sqrt)
                        run(inv_q[:, g % 2, :], inv2[:, 0:TILES * GH], ACT.Sqrt).then_inc(rooted, 1)
                    if g == 3 and prev:
                        need(act, ln_scaled, n)
                        need(act, z_done, n)
                        run(ln_aff[:], ln_out[:], ACT.Identity, bias=vff[:, 1:2]).then_inc(ln_done, 1)
                    if has(g, 3, prev, cur):
                        if g == 3:
                            need(act, o_proj, n)
                        save_values(0)
                        save_values(1)
                    if g == 2 and cur:
                        place(u - 2)
                        save_v(2)
                        save_v(3)
                    if g == 2 and prev:
                        need(act, centred_set, n)
                        run(ln_sq[:], centred[:], ACT.Square).then_inc(ln_squared, 1)
                    if g == 3 and prev:
                        for c, bank in enumerate((pq[:, 0, :], pq[:, 1, :], pk[:, 0, :])):
                            m = CHUNKS[c][1]
                            need(act, gates_up, NC * (n - 1) + c + 1)
                            run(gate[0:m, c, :], bank[0:m, :], ACT.Gelu, bias=vff[0:m, 3 + NC + c:4 + NC + c])\
                                .then_inc(gelu_done, 1)
                    if g == 3 and cur:
                        need(act, v_proj, 2 * u + 2)
                        shift_in(n + 1, n - 1)
                        place(u - 2)

            with act.Fori(0, B) as b:
                layer_norm(b)
            act.wait_ge(n_done, B + 1)
            shift_in(0, 0)
            emit(body, act, 0)
            with act.Fori(0, B) as b:
                layer_norm(B + b)
            with act.Fori(0, B) as b:
                attention(b)
            with act.Fori(0, B) as b:
                layer_norm(2 * B + b)
            act.wait_ge(n_done, 3 * B + 1)
            shift_in(ITERS, ITERS)
            emit(body, act, ITERS)

        @block.vector
        def _(dve):
            v = nc.vector
            v.memset(khat[:], 0.0).then_inc(cleared, 1)
            v.memset(band[:], 0.0).then_inc(cleared, 1)
            v.memset(xs[:], 0.0).then_inc(cleared, 1)
            v.memset(z_shift[:], 0.0).then_inc(cleared, 1)
            v.memset(mean_w[:], 1.0 / D).then_inc(cleared, 1)
            v.memset(k_split[:].bitcast(F32), 0.0).then_inc(cleared, 1)
            v.memset(ln_split[:].bitcast(F32), 0.0).then_inc(cleared, 1)
            for i, primed in enumerate((z_done, n_done, a_done)):
                v.memset(primer[:, i:i + 1], 0.0).then_inc(primed, 1)
            dve.wait_ge(consts_in, CONSTS)
            v.tensor_copy(identity16[:], identity[:]).then_inc(consts_cast, 1)
            v.tensor_copy(mask16[:], squares[:, 0:2, :]).then_inc(consts_cast, 1)
            v.tensor_copy(row_sel[:].rearrange("p q m -> p (q m)"), squares[:, 2, :]).then_inc(consts_cast, 1)
            dve.wait_ge(cleared, 7)

            def rows_of(split, value, rows, low, turned_, count):
                v.tensor_tensor(split[:, :, GH:2 * GH], value, split[:, :, 0:GH].bitcast(F32), ALU.subtract)\
                    .then_inc(low, 1)
                need(dve, low, count)
                v.transpose(turned[:], split[:].bitcast(F32).rearrange("p j r -> p (j r)")).then_inc(turned_, 1)
                need(dve, turned_, count)
                return v.tensor_copy(rows[:], turned[:])

            def layer_norm(k, src, dst):
                need(dve, n_mean, k + 1)
                need(dve, n_done, k + 1)
                v.tensor_tensor(centred[:], src, pM[:], ALU.subtract).then_inc(n_centred, 1)
                need(dve, n_var, k + 1)
                v.tensor_scalar(ln_var[:], pM[:, 0:TILES], LN_EPS, None, ALU.add).then_inc(n_eps, 1)
                need(dve, n_eps, k + 1)
                v.reciprocal(ln_inv[:], ln_var[:]).then_inc(n_inv, 1)
                need(dve, n_rstd, k + 1)
                rows_of(ln_split, ln_rstd[:].unsqueeze(2).to_broadcast([P, TILES, GH]), ln_rows, n_low, n_turned, k + 1)\
                    .then_inc(n_rowed, 1)
                need(dve, n_spread, k + 1)
                v.tensor_tensor(dst, centred[:], pM[:], ALU.mult).then_inc(n_done, 1)

            def attention(b):
                need(dve, a_kqv, b + 1)
                v.tensor_copy(squares[:, 1, :], p4[:, 1, :]).then_inc(a_q, 1)
                need(dve, a_u, b + 1)
                v.tensor_copy(sumsq[:, 0, :], pO[:]).then_inc(a_us, 1)
                need(dve, a_scores, b + 1)
                v.tensor_reduce(row_max[:, 0:TILES], p4[:], AX_X, ALU.max, negate=True).then_inc(a_max, 1)
                need(dve, a_exp, b + 1)
                v.reduce_sum(row_sum[:, 0:TILES], q_terms[:], AX_X).then_inc(a_sum, 1)
                need(dve, a_sum, b + 1)
                v.reciprocal(inv_sum[:, 0:TILES], row_sum[:, 0:TILES]).then_inc(a_isum, 1)
                need(dve, a_isum, b + 1)
                v.tensor_tensor(q_terms[:], q_terms[:], inv_sum[:, 0:TILES].unsqueeze(2).to_broadcast([P, TILES, S]),
                                ALU.mult).then_inc(a_norm, 1)
                need(dve, a_tr, b + 1)
                v.tensor_copy(k_terms[:, 2:4, :], p4[:, 2:4, :]).then_inc(a_trd, 1)
                need(dve, a_out, b + 1)
                v.tensor_tensor(batch(X, b), batch(X, b), pS[:, 0, :], ALU.add).then_inc(a_done, 1)

            def body(n, prev, cur, st):
                if cur:
                    need(dve, k_prod, 4 * n)
                    layer = n // B - LAYERS * st
                    v.tensor_copy(vqk[:], vecs[:, bass.ds(layer, 1), 0:4].rearrange("p a c -> p (a c)"))\
                        .then_inc(vqk_set, 1)
                    need(dve, vqk_set, n + 1)
                for g in range(GROUPS):
                    u = 4 * n + g

                    def transpose_probs():
                        need(dve, normed, u - 1)
                        need(dve, placed, u - 2)
                        v.transpose(probs_t[:].rearrange("p j h b t -> p (j h b t)"),
                                    probs[:].rearrange("p r s -> p (r s)")).then_inc(transposed, 1)

                    def rows_of_keys():
                        need(dve, rooted, u + 1)
                        need(dve, spread_k, u)
                        rows_of(k_split, inv_k[:], k_rows, k_low, k_turned, u + 1).then_inc(k_rowed, 1)

                    def terms(dst, src, vcol, cos, sin, which=(0, 1, 2, 3)):
                        for i in which:
                            half, table = ((0, cos), (1, sin), (1, cos), (0, sin))[i]
                            last = v.scalar_tensor_tensor(out=dst[:, i, :], in0=src[:, half, :],
                                                          scalar=vqk[:, vcol + half:vcol + half + 1], in1=table,
                                                          op0=ALU.mult, op1=ALU.mult)
                        return last

                    if cur:
                        need(dve, squared, 2 * u + 1)
                        need(dve, k_rot, u)
                        terms(k_terms, pk, 2, ck, sk).then_inc(k_prod, 1)
                    if g == 3 and prev:
                        need(dve, var_done, n)
                        v.tensor_scalar(ln_var[:], pO[:, 0:TILES], LN_EPS, None, ALU.add).then_inc(var_eps, 1)
                        need(dve, var_eps, n)
                        v.reciprocal(ln_inv[:], ln_var[:]).then_inc(var_inverted, 1)
                    if cur:
                        need(dve, squared, 2 * u + 2)
                        need(dve, q_rot, u)
                        terms(q_terms, pq, 0, cq, sq_, (0, 1))
                    if g == 3 and prev:
                        need(dve, rstd_set, n)
                        rows_of(ln_split, ln_rstd[:].unsqueeze(2).to_broadcast([P, TILES, GH]), ln_rows, rstd_low,
                                rstd_turned, n).then_inc(rstd_rowed, 1)
                    if has(g, 2, prev, cur):
                        need(dve, expd, u - 1)
                        v.reduce_sum(row_sum[:], probs[:], AX_X).then_inc(rows_summed, 1)
                        need(dve, rows_summed, u - 1)
                        v.reciprocal(inv_sum[:], row_sum[:]).then_inc(sums_inverted, 1)
                    if cur:
                        need(dve, summed, u + 1)
                        need(dve, clamped, u)
                        v.transpose(tok_sums[:].rearrange("p a b -> p (a b)"), pM[:, 0:2 * P]).then_inc(by_token, 1)
                        need(dve, by_token, u + 1)
                        need(dve, inverted, u)
                        v.tensor_scalar(norm2[:].rearrange("p (a h) -> p a h", h=GH), tok_sums[:, :, 0:GH],
                                        NORM_EPS ** 2, None, ALU.max).then_inc(clamped, 1)
                        need(dve, clamped, u + 1)
                        need(dve, rooted, u)
                        v.reciprocal(inv2[:], norm2[:]).then_inc(inverted, 1)
                    if g == 3 and prev:
                        need(dve, rstd_spread, n)
                        v.scalar_tensor_tensor(out=ln_out[:], in0=centred[:], scalar=vff[:, 0:1], in1=pO[:],
                                               op0=ALU.mult, op1=ALU.mult).then_inc(ln_scaled, 1)
                    if cur:
                        terms(q_terms, pq, 0, cq, sq_, (2, 3)).then_inc(q_prod, 1)
                    if g in (0, 3) and cur:
                        rows_of_keys()
                    if has(g, 1, prev, cur):
                        need(dve, scored, u)
                        scores = pS[:].rearrange("p b (r s) -> p (b r) s", s=2 * WIN)
                        v.reduce_max(row_max[:], scores, AX_X).then_inc(maxed, 1)
                    if g in (1, 2) and cur:
                        rows_of_keys()
                    if g > 0 and has(g, 2, prev, cur):
                        transpose_probs()
                    if cur:
                        need(dve, spread_k, u + 1)
                        need(dve, k_rot, u + 1)
                        need(dve, khat_in, 16 * GH * u)
                        v.tensor_tensor(k_normed[:], k_rotated[:], K_BANK[g][:].unsqueeze(1).to_broadcast([P, 2, S]),
                                        ALU.mult).then_inc(k_norm, 1)
                    if g == 0 and prev:
                        transpose_probs()
                    if has(g, 1, prev, cur):
                        need(dve, maxed, u)
                        need(dve, transposed, u - 1)
                        v.tensor_tensor(probs[:], scores, row_max[:].unsqueeze(2).to_broadcast([P, TILES * GH, 2 * WIN]),
                                        ALU.subtract).then_inc(shifted, 1)
                    if g == 2 and prev:
                        need(dve, z_done, n)
                        layer = (n - 1) // B - LAYERS * st
                        v.tensor_copy(vff[:], vecs[:, bass.ds(layer, 1), 4:].rearrange("p a c -> p (a c)"))\
                            .then_inc(vff_set, 1)
                        need(dve, o_proj, n)
                        v.tensor_tensor(z_mid[:], batch(Z, n - 1), pM[:], ALU.add).then_inc(z_mid_set, 1)
                        need(dve, z_mid_set, n)
                        v.tensor_copy(z_shift[0:D // 2, :], z_mid[0:D // 2, :])
                        v.tensor_copy(z_shift[D // 2:D, 1:S], z_mid[D // 2:D, 0:S - 1]).then_inc(z_shifted, 1)
                        need(dve, z_shifted, n)
                        need(dve, mean_done, n)
                        v.tensor_tensor(centred[:], z_shift[:], pO[:], ALU.subtract).then_inc(centred_set, 1)
                    if g == 3 and prev:
                        need(dve, vff_set, n)
                        for c, bank in enumerate((pk[:, 1, :], pO[:], pM[:])):
                            m = CHUNKS[c][1]
                            need(dve, gelu_done, NC * (n - 1) + c + 1)
                            need(dve, values_up, NC * (n - 1) + c + 1)
                            v.scalar_tensor_tensor(out=hidden[0:m, c, :], in0=bank[0:m, :], scalar=vff[0:m, 3 + c:4 + c],
                                                   in1=gate[0:m, c, :], op0=ALU.add, op1=ALU.mult)\
                                .then_inc(hidden_set, 1)
                        need(dve, ff_down, n)
                        v.scalar_tensor_tensor(out=batch(Z, n - 1), in0=pq[:, 0, :], scalar=vff[:, 2:3], in1=z_mid[:],
                                               op0=ALU.add, op1=ALU.add).then_inc(z_done, 1)

            with dve.Fori(0, B) as b:
                layer_norm(b, batch(X, b), batch(Z, b))
            dve.wait_ge(n_done, B + 1)
            emit(lambda n, prev, cur: body(n, prev, cur, 0), dve, 0)
            dve.wait_ge(z_done, ITERS + 1)
            v.scalar_tensor_tensor(out=X[:], in0=Z[:], scalar=0.5, in1=X[:], op0=ALU.mult, op1=ALU.add)\
                .then_inc(x_updated, 1)
            dve.wait_ge(x_updated, 1)
            with dve.Fori(0, B) as b:
                layer_norm(B + b, batch(X, b), batch(Z, b))
            with dve.Fori(0, B) as b:
                attention(b)
            dve.wait_ge(a_done, B + 1)
            with dve.Fori(0, B) as b:
                layer_norm(2 * B + b, batch(X, b), batch(Z, b))
            dve.wait_ge(n_done, 3 * B + 1)
            emit(lambda n, prev, cur: body(n, prev, cur, 1), dve, ITERS)
            dve.wait_ge(z_done, 2 * ITERS + 1)
            v.scalar_tensor_tensor(out=X[:], in0=Z[:], scalar=0.5, in1=X[:], op0=ALU.mult, op1=ALU.add)\
                .then_inc(x_updated, 1)

        @block.gpsimd
        def _(pool):
            tt = nc.gpsimd.tensor_tensor

            def body(n, prev, cur):
                for g in range(GROUPS):
                    u = 4 * n + g
                    if has(g, 2, prev, cur):
                        need(pool, shifted, u - 1)
                        need(pool, rooted, u - 1)
                        tt(probs[:], probs[:], inv_q[:, g % 2, :].unsqueeze(2).to_broadcast([P, TILES * GH, 2 * WIN]),
                           ALU.mult).then_inc(scaled, 1)
                    if cur:
                        for i, qk in enumerate((1, 0)):
                            need(pool, squared, 2 * u + i + 1)
                            need(pool, summed, u)
                            tt(sumsq[:, qk, :], squares[:, 2 * i, :], squares[:, 2 * i + 1, :], ALU.add)\
                                .then_inc(paired, 1)
                    if has(g, 2, prev, cur):
                        need(pool, sums_inverted, u - 1)
                        tt(probs[:], probs[:], inv_sum[:].unsqueeze(2).to_broadcast([P, TILES * GH, 2 * WIN]), ALU.mult)\
                            .then_inc(normed, 1)
                    if cur:
                        need(pool, k_prod, u + 1)
                        need(pool, k_norm, u)
                        tt(k_rotated[:, 0, :], k_terms[:, 0, :], k_terms[:, 1, :], ALU.subtract)
                        tt(k_rotated[:, 1, :], k_terms[:, 2, :], k_terms[:, 3, :], ALU.add).then_inc(k_rot, 1)
                        need(pool, q_prod, u + 1)
                        need(pool, scored, u - 1)
                        qr = q_rotated[:, g % 2, :, :]
                        tt(qr[:, 0, :], q_terms[:, 0, :], q_terms[:, 1, :], ALU.subtract)
                        tt(qr[:, 1, :], q_terms[:, 2, :], q_terms[:, 3, :], ALU.add).then_inc(q_rot, 1)

            emit(body, pool, 0)
            pool.wait_ge(a_done, B + 1)
            emit(body, pool, ITERS)


def kernel(**inputs):
    import numpy as np
    import concourse.bacc as bacc
    from concourse.bass_utils import run_bass_kernel_spmd

    a = {k: np.asarray(x) for k, x in inputs.items()}
    f = lambda name: a["L0_ffn_" + name]
    w = f("Wqkv").reshape(LAYERS, D, 3, GROUPS, GH, 2, HALF)
    vec = np.zeros((P, LAYERS, VEC), np.float32)
    for c, name in ((0, "q_scale"), (2, "k_scale")):
        halves = f(name).reshape(LAYERS, 2, HALF).transpose(2, 0, 1)
        vec[:, :, c:c + 2] = np.tile(halves, (GH, 1, 1))
    vec[:, :, 4], vec[:, :, 5], vec[:, :, 6] = f("ln_g").T, f("ln_b").T, f("b2").T
    b1 = f("b1")
    w2 = np.zeros((LAYERS, P, NC, D), np.float32)
    for c, (at, m) in enumerate(CHUNKS):
        vec[0:m, :, 7 + c] = b1[:, at:at + m].T
        vec[0:m, :, 7 + NC + c] = b1[:, FF + at:FF + at + m].T
        w2[:, 0:m, c] = f("W2")[:, at:at + m]

    half = np.arange(0, DH, 2, dtype=np.float32)
    inv_freq = (1.0 / np.float32(10000.0) ** (half / np.float32(DH))).astype(np.float32)
    t = np.arange(S, dtype=np.float32)
    angle = (inv_freq[:, None] * t[None, :]).astype(np.float32)
    base = ((half + np.float32(0.4 * DH)) / np.float32(1.4 * DH)).astype(np.float32)
    scale = (base[:, None] ** ((t - S // 2) / (WIN // 2))[None, :]).astype(np.float32)
    cos, sin = np.cos(angle), np.sin(angle)
    rot = np.stack([cos * scale, sin * scale, cos * (1 / scale), sin * (1 / scale)], 1).astype(np.float32)
    rot = np.tile(rot, (GH, 1, 1))
    r, s = np.arange(P)[:, None] % WIN, np.arange(2 * WIN)[None, :]
    allowed = (s >= r) & (s <= r + WIN)
    mask = np.where(allowed, 0.0, MASKED).astype(np.float32)[:, None, None, :]
    mask = np.broadcast_to(mask, (P, TILES, GH, 2 * WIN)).copy()
    mask[0:WIN, 0, :, 0:WIN] = MASKED
    sel = (np.arange(P)[:, None] // HALF == np.arange(WIN)[None, :]).astype(np.float32)
    row = np.arange(P)[:, None] % WIN
    spread_sel = (row < 2 * GH) & (row % GH == np.arange(P)[None, :] // HALF)
    spread_sel = np.stack([spread_sel & (np.arange(P)[:, None] // WIN == q) for q in range(WPT)], 1)

    arrays = {
        "x_t": a["L0_attn_x"].transpose(2, 0, 1),
        "w_qk": w[:, :, 0:2].transpose(0, 3, 1, 2, 5, 4, 6).reshape(LAYERS, GROUPS, D, 4 * P),
        "w_v": f("Wqkv")[:, :, 2 * HEADS * DH:],
        "w_o": f("Wo").reshape(LAYERS, PAIRS, P, D).transpose(0, 2, 1, 3).reshape(LAYERS, P, PAIRS * D),
        "w_1": f("W1"),
        "w_2": w2.reshape(LAYERS, P, NC * D),
        "vec": vec,
        "rot": rot,
        "mask": mask.reshape(P, 2, S),
        "ident": np.eye(P, dtype=np.float32),
        "a_w": np.concatenate([a["L0_attn_W" + c].T for c in "kqvab"], 1),
        "sel": sel,
        "spread_sel": spread_sel.reshape(P, WPT * P).astype(np.float32),
    }
    arrays = {k: np.ascontiguousarray(x) for k, x in arrays.items()}
    nc = bacc.Bacc("TRN2", target_bir_lowering=False, num_devices=1)
    args = {k: nc.dram_tensor(k + "_dram", x.shape, F32, kind="ExternalInput").ap() for k, x in arrays.items()}
    out = nc.dram_tensor("out_dram", (P, B, S), F32, kind="ExternalOutput").ap()
    macaron(nc, **args, out=out)
    r = run_bass_kernel_spmd(nc, [{k + "_dram": x for k, x in arrays.items()}], core_ids=[0])
    return np.ascontiguousarray(r.results[0]["out_dram"].transpose(1, 2, 0))
```

```python
from contextlib import ExitStack

import concourse.bass as bass
from concourse import mybir

F32 = mybir.dt.float32
F32R = mybir.dt.float32r
BF16 = mybir.dt.bfloat16
ALU = mybir.AluOpType
ACT = mybir.ActivationFunctionType
AX_X = mybir.AxisListType.X

P = 128
B, S, D = 4, 512, 128
LAYERS, HEADS, DH, WIN = 6, 16, 64, 32
HALF = DH // 2
GH = P // HALF
GROUPS = HEADS // GH
TILES = S // P
WPT = P // WIN
PAIRS = HEADS // 2
PLACED_BY_VECTOR = 2
V_COLS = GH * DH
V_CHUNKS = (2, 2, 4, 0)
FF = D * 4 * 2 // 3
CHUNKS = [(c, min(P, FF - c)) for c in range(0, FF, P)]
NC = len(CHUNKS)
ITERS = LAYERS * B
SPAN = P + WIN
QK_SCALE = 8.0
LN_EPS = 1e-5
NORM_EPS = 1e-12
MASKED = -1e30
VEC = 6 + 2 * NC + 1


def need(eng, sem, count):
    if not isinstance(count, int) or count > 0:
        eng.wait_ge(sem, count)


def macaron(nc, x_t, w_qk, w_v, w_o, w_1, w_2, vec, rot, mask, ident, a_w, sel, spread_sel, out):
    with ExitStack() as ctx:
        def sb(name, shape, dt=F32):
            return ctx.enter_context(nc.sbuf_tensor(name, shape, dt))

        def ps(name, shape):
            return ctx.enter_context(nc.psum_tensor(name, shape, F32))

        def sem(name):
            return ctx.enter_context(nc.semaphore(name))

        X = sb("X", [P, B, S])
        Z = sb("Z", [P, B, S])
        wqk = sb("wqk", [P, GROUPS, 4, P])
        wv = sb("wv", [P, HEADS * DH])
        wo = sb("wo", [P, PAIRS, D])
        w1 = sb("w1", [P, 2 * FF])
        w2 = sb("w2", [P, NC, D])
        attn_w = sb("attn_w", [P, 5, D])
        vecs = sb("vecs", [P, LAYERS, VEC])
        vqk = sb("vqk", [P, 4])
        vff = sb("vff", [P, VEC - 4])
        rotary = sb("rotary", [P, 4, S])
        cq, sq_, ck, sk = (rotary[:, i, :] for i in range(4))
        identity = sb("identity", [P, P])
        identity16 = sb("identity16", [P, P], BF16)
        mask16 = sb("mask16", [P, 2, 2 * GH * 2 * WIN], BF16)
        head_sel = sb("head_sel", [P, WIN])
        mean_w = sb("mean_w", [P, P])
        xs = sb("xs", [P, S])
        squares = sb("squares", [P, 4, S])
        sumsq = sb("sumsq", [P, 2, S])
        q_terms = sb("q_terms", [P, 4, S])
        k_terms = sb("k_terms", [P, 4, S])
        q_rotated = sb("q_rotated", [P, 2, 2, S])
        k_rotated = sb("k_rotated", [P, 2, S])
        k_normed = sb("k_normed", [P, 2, S])
        khat = sb("khat", [P, 2, GH, WIN + S])
        tok_sums = sb("tok_sums", [P, 2 * TILES, WIN])
        norm2 = sb("norm2", [P, 2 * TILES * GH])
        inv2 = sb("inv2", [P, 2 * TILES * GH])
        inv_q = sb("inv_q", [P, 2, TILES * GH])
        inv_k = sb("inv_k", [P, TILES, GH])
        k_split = sb("k_split", [P, TILES, WIN], F32R)
        turned = sb("turned", [P, B, TILES * WIN])
        k_rows = sb("k_rows", [P, TILES * WIN], F32R)
        ln_split = sb("ln_split", [P, B, TILES, WIN], F32R)
        ln_rows = sb("ln_rows", [P, B, TILES * WIN], F32R)
        row_sel = sb("row_sel", [P, WPT, P], F32R)
        row_max = sb("row_max", [P, TILES * GH])
        row_sum = sb("row_sum", [P, TILES * GH])
        inv_sum = sb("inv_sum", [P, TILES * GH])
        probs = sb("probs", [P, TILES * GH, 2 * WIN])
        probs_t = sb("probs_t", [P, TILES, GH, 2, WIN])
        band = sb("band", [P, TILES, GH, SPAN])
        V = sb("V", [P, TILES, HEADS * DH])
        heads_out = sb("heads_out", [P, PAIRS, S])
        z_mid = sb("z_mid", [P, S])
        z_shift = sb("z_shift", [P, S])
        centred = sb("centred", [P, S])
        ln_sq = sb("ln_sq", [P, S])
        ln_var = sb("ln_var", [P, B, TILES])
        ln_inv = sb("ln_inv", [P, B, TILES])
        ln_rstd = sb("ln_rstd", [P, B, TILES])
        ln_out = sb("ln_out", [P, S])
        ln_aff = sb("ln_aff", [P, S])
        gate = sb("gate", [P, NC, S])
        hidden = sb("hidden", [P, NC, S])

        primer = sb("primer", [P, 3])

        p4 = ps("p4", [P, 4, S])
        pq, pk = p4[:, 0:2, :], p4[:, 2:4, :]
        pS = ps("pS", [P, 2, S])
        pO = ps("pO", [P, S])
        pM = ps("pM", [P, S])

        V_BANK = (pO, pM, pO, pM)
        O_BANK = ((pO[:], pM[:]), (pO[:], pM[:]), (pM[:], pO[:]), (pk[:, 0, :], pk[:, 1, :]))
        K_BANK = (pO[:], pO[:], pO[:], pq[:, 1, :])
        GATE_BANK = (pM[:], pO[:], pq[:, 0, :])
        UP_BANK = (pk[:, 0, :], pk[:, 1, :], pq[:, 1, :])
        DOWN_BANK = pM[:]

        state_in, consts_in, consts_cast, cleared = sem("state_in"), sem("consts_in"), sem("consts_cast"), sem("cleared")
        wqk_in = [sem(f"wqk_in{g}") for g in range(GROUPS)]
        wv_in, wo_in, wff_in = sem("wv_in"), sem("wo_in"), sem("wff_in")
        xs_ready = sem("xs_ready")
        q_proj, k_proj, squared, paired = sem("q_proj"), sem("k_proj"), sem("squared"), sem("paired")
        q_prod, k_prod, q_rot, k_rot = sem("q_prod"), sem("k_prod"), sem("q_rot"), sem("k_rot")
        summed, by_token, clamped, inverted, rooted = (
            sem("summed"), sem("by_token"), sem("clamped"), sem("inverted"), sem("rooted"))
        k_low, k_rowed, rstd_low, rstd_rowed = sem("k_low"), sem("k_rowed"), sem("rstd_low"), sem("rstd_rowed")
        k_turned, rstd_turned, n_turned = sem("k_turned"), sem("rstd_turned"), sem("n_turned")
        spread_k, k_norm, khat_in = sem("spread_k"), sem("k_norm"), sem("khat_in")
        scored, maxed, shifted, scaled, expd = (sem("scored"), sem("maxed"), sem("shifted"), sem("scaled"), sem("expd"))
        rows_summed, sums_inverted, normed = sem("rows_summed"), sem("sums_inverted"), sem("normed")
        transposed, placed, placed_too, valued, o_saved = sem("transposed"), sem("placed"), sem("placed_too"), sem("valued"), sem("o_saved")
        v_proj, v_saved = sem("v_proj"), sem("v_saved")
        vqk_set, vff_set = sem("vqk_set"), sem("vff_set")
        o_proj, z_mid_set, z_shifted = sem("o_proj"), sem("z_mid_set"), sem("z_shifted")
        mean_done, centred_set, ln_squared, var_done = (sem("mean_done"), sem("centred_set"), sem("ln_squared"), sem("var_done"))
        var_eps, var_inverted, rstd_set, rstd_spread = (sem("var_eps"), sem("var_inverted"), sem("rstd_set"), sem("rstd_spread"))
        ln_scaled, ln_done = sem("ln_scaled"), sem("ln_done")
        gates_up, values_up, gelu_done, hidden_set = (sem("gates_up"), sem("values_up"), sem("gelu_done"), sem("hidden_set"))
        ff_down, z_done = sem("ff_down"), sem("z_done")
        n_mean, n_centred, n_squared, n_var, n_eps, n_inv, n_rstd, n_low, n_rowed, n_spread, n_done = (
            sem("n_" + s) for s in ("mean", "centred", "squared", "var", "eps", "inv", "rstd", "low", "rowed", "spread", "done"))
        x_updated = sem("x_updated")
        a_kqv, a_k, a_v, a_q, a_ak, a_u, a_aks, a_us, a_scores, a_max, a_exp = (
            sem("a_" + s) for s in ("kqv", "k", "v", "q", "ak", "u", "aks", "us", "scores", "max", "exp"))
        a_sum, a_isum, a_norm, a_tr, a_trs, a_trd, a_out, a_done = (
            sem("a_" + s) for s in ("sum", "isum", "norm", "tr", "trs", "trd", "out", "done"))
        out_stored = sem("out_stored")

        block = ctx.enter_context(nc.Block())
        CONSTS = 6 * 16

        def has(g, back, prev, cur):
            return cur if g >= back else prev

        def batch(t, n):
            return t[:, bass.ds(n % B, 1), :].rearrange("p a s -> p (a s)")

        def emit(body, eng, n0):
            body(n0, prev=False, cur=True)
            with eng.Fori(n0 + 1, n0 + ITERS) as n:
                body(n, prev=True, cur=True)
            body(n0 + ITERS, prev=True, cur=False)

        def rows_loop(step, eng):
            step(0, prev=False, cur=True)
            with eng.Fori(1, B) as b:
                step(b, prev=True, cur=True)
            step(B, prev=True, cur=False)

        @block.sync
        def _(sp):
            for dst, src in ((X[:], x_t), (squares[:, 2, :], spread_sel)):
                sp.dma_start(dst, src).then_inc(state_in, 16)
            for dst, src in ((identity[:], ident), (squares[:, 0:2, :], mask), (head_sel[:], sel),
                             (vecs[:], vec), (rotary[:], rot), (attn_w[:].rearrange("p a m -> p (a m)"), a_w)):
                sp.dma_start(dst, src).then_inc(consts_in, 16)

            def load_qk(layer, g):
                sp.dma_start(wqk[:, g, :, :].rearrange("p a m -> p (a m)"),
                             w_qk[bass.ds(layer, 1), g, :, :].rearrange("a p m -> p (a m)")).then_inc(wqk_in[g], 16)

            def load_v(layer):
                sp.dma_start(wv[:], w_v[bass.ds(layer, 1), :, :].rearrange("a p m -> p (a m)")).then_inc(wv_in, 16)

            def load_o(layer):
                sp.dma_start(wo[:].rearrange("p a m -> p (a m)"),
                             w_o[bass.ds(layer, 1), :, :].rearrange("a p m -> p (a m)")).then_inc(wo_in, 16)

            def load_ff(layer):
                sp.dma_start(w1[:], w_1[bass.ds(layer, 1), :, :].rearrange("a p m -> p (a m)")).then_inc(wff_in, 16)
                sp.dma_start(w2[:].rearrange("p a m -> p (a m)"),
                             w_2[bass.ds(layer, 1), :, :].rearrange("a p m -> p (a m)")).then_inc(wff_in, 16)

            for g in range(GROUPS):
                load_qk(0, g)
            load_v(0)
            load_o(0)
            load_ff(0)
            sp.wait_ge(cleared, 7)

            def spread(u):
                need(sp, k_norm, u + 1)
                for h in range(GH):
                    sp.dma_start(khat[HALF * h:HALF * (h + 1), :, h, WIN:],
                                 k_normed[HALF * h:HALF * (h + 1), :, :]).then_inc(khat_in, 16)

            def layer_loads(lay, first, last):
                for row in range(B):
                    for g in range(GROUPS):
                        spread(4 * (B * lay + row) + g)
                        if row == 0 and g == 3 and not first:
                            load_o(lay % LAYERS)
                        if row == 1 and g == 0 and not first:
                            load_ff(lay % LAYERS)
                        if row == B - 1 and not last:
                            load_qk((lay + 1) % LAYERS, g)
                            if g == 3:
                                load_v((lay + 1) % LAYERS)

            layer_loads(0, True, False)
            with sp.Fori(1, 2 * LAYERS - 1) as lay:
                layer_loads(lay, False, False)
            layer_loads(2 * LAYERS - 1, False, True)
            sp.wait_ge(x_updated, 2)
            sp.dma_start(out, X[:]).then_inc(out_stored, 16)
            sp.wait_ge(out_stored, 16)

        @block.tensor
        def _(pe):
            mm = nc.tensor.matmul
            pe.wait_ge(state_in, 2 * 16)
            pe.wait_ge(consts_cast, 1)
            pe.wait_ge(cleared, 7)

            def spread(rows, bank):
                by_window = bank.rearrange("p (j q t) -> p j q t", j=TILES, q=WPT)
                for q in range(WPT):
                    last = mm(by_window[:, :, q, :], row_sel[:, q, :], rows, start=True, stop=True)
                return last

            def layer_norms(k):
                need(pe, n_done, B * k + 1)
                for b in range(B):
                    mm(p4[:, b, :], mean_w[:], X[:, b, :], start=True, stop=True).then_inc(n_mean, 1)
                for b in range(B):
                    need(pe, n_squared, B * k + b + 1)
                    for j in range(TILES):
                        last = mm(pM[:, TILES * b + j:TILES * b + j + 1], k_terms[:, b, P * j:P * (j + 1)], mean_w[:, 0:1],
                                  start=True, stop=True)
                last.then_inc(n_var, 1)
                need(pe, n_rowed, k + 1)
                for b in range(B):
                    spread(ln_rows[:, b, :], p4[:, b, :]).then_inc(n_spread, 1)

            def attention(b, prev, cur):
                wk_, wq_, wv_, wa_, wb_ = (attn_w[:, i, :] for i in range(5))
                if cur:
                    need(pe, a_us, b)
                    need(pe, a_done, b)
                    mm(pS[:, 0, :], wk_, batch(Z, b), start=True, stop=True)
                    mm(pS[:, 1, :], wq_, batch(Z, b), start=True, stop=True)
                    mm(pM[:], wv_, batch(Z, b), start=True, stop=True).then_inc(a_kqv, 1)
                    need(pe, a_k, b + 1)
                    need(pe, a_aks, b)
                    mm(pO[:], wa_, squares[:, 0, :], start=True, stop=True).then_inc(a_ak, 1)
                if prev:
                    for i in range(TILES):
                        need(pe, a_norm, TILES * (b - 1) + i + 1)
                        for j in range(TILES):
                            last = mm(p4[:, j, P * i:P * (i + 1)], q_terms[:, i, P * j:P * (j + 1)], identity[:],
                                      start=True, stop=True)
                    last.then_inc(a_tr, 1)
                    need(pe, a_trs, b)
                    need(pe, a_trd, b)
                    if cur:
                        need(pe, a_v, b + 1)
                    for j in range(TILES):
                        last = mm(pM[:], sumsq[:, 0, P * j:P * (j + 1)], k_terms[:, j, :],
                                  start=(j == 0), stop=(j == TILES - 1))
                    last.then_inc(a_out, 1)
                if cur:
                    need(pe, a_v, b + 1)
                    for j in range(TILES):
                        last = mm(pS[:, 0, P * j:P * (j + 1)], squares[:, 2, P * j:P * (j + 1)], wb_, start=True, stop=True)
                    last.then_inc(a_u, 1)
                    need(pe, a_aks, b + 1)
                    need(pe, a_q, b + 1)
                    for i in range(TILES):
                        mm(p4[:, i, :], squares[:, 1, P * i:P * (i + 1)], squares[:, 3, :], start=True, stop=True)\
                            .then_inc(a_scores, 1)

            def body(n, prev, cur, st):
                for g in range(GROUPS):
                    u = 4 * n + g

                    def project(bank, w, done):
                        mm(bank[:, 0, :], wqk[:, g, w, :], xs[:], start=True, stop=True)
                        mm(bank[:, 1, :], wqk[:, g, w + 1, :], xs[:], start=True, stop=True).then_inc(done, 1)

                    def project_v(c):
                        heads = V_COLS * (g + c // 2)
                        for jj in range(2):
                            j = 2 * (c % 2) + jj
                            last = mm(V_BANK[c][:, V_COLS * jj:V_COLS * (jj + 1)],
                                      xs[:, P * j:P * (j + 1)], wv[:, heads:heads + V_COLS], start=True, stop=True)
                        last.then_inc(v_proj, 1)

                    def values(pair):
                        bank = O_BANK[g][pair]
                        for hh in range(2):
                            h = 2 * pair + hh
                            feat = (GH * ((g - 3) % GROUPS) + h) * DH
                            for j in range(TILES):
                                wide = min(SPAN, S - P * j)
                                last = mm(bank[DH * hh:DH * (hh + 1), P * j:P * j + wide],
                                          V[:, j, feat:feat + DH], band[:, j, h, 0:wide],
                                          start=(j == 0), stop=(j == TILES - 1), skip_group_check=True)
                        last.then_inc(valued, 1)

                    def scores(half):
                        qr = q_rotated[:, (g - 1) % 2, :, :]
                        mm(pS[:, half, :], identity16[:], mask16[:, half, :], start=True, stop=False,
                           skip_group_check=True)
                        for j in range(2):
                            cols = j * GH * 2 * WIN
                            for ab in range(2):
                                for q in range(WPT):
                                    w = WPT * (2 * half + j) + q
                                    last = mm(pS[WIN * q:WIN * (q + 1), half, cols:cols + GH * 2 * WIN],
                                              qr[:, ab, WIN * w:WIN * (w + 1)],
                                              khat[:, ab, :, WIN * w:WIN * (w + 2)],
                                              start=False, stop=(ab == 1), skip_group_check=True)
                        return last

                    def spread_keys():
                        need(pe, k_rowed, u + 1)
                        if g < 3:
                            need(pe, o_saved, 2 * u - 5)
                        else:
                            need(pe, q_prod, u + 1)
                        spread(k_rows[:], K_BANK[g]).then_inc(spread_k, 1)

                    def lengths():
                        need(pe, paired, 2 * u + 2)
                        need(pe, v_saved, 2 * u + 2)
                        for qk in range(2):
                            by_window = sumsq[:, qk, :].rearrange("p (j q t) -> p j q t", j=TILES, q=WPT)
                            for q in range(WPT):
                                last = mm(pM[WIN * q:WIN * (q + 1), P * qk:P * (qk + 1)], head_sel[:],
                                          by_window[:, :, q, :], start=True, stop=True, skip_group_check=True)
                        last.then_inc(summed, 1)

                    if cur:
                        need(pe, xs_ready, n + 1 + st)
                        need(pe, wqk_in[g], 16 * (n // B + 1))
                        need(pe, k_prod, u)
                        project(pk, 2, k_proj)
                        need(pe, q_prod, u)
                        if g == 0:
                            need(pe, k_norm, u)
                        project(pq, 0, q_proj)
                    if g < 3 and cur:
                        need(pe, wv_in, 16 * (n // B + 1))
                        need(pe, k_norm, u)
                        need(pe, o_saved, 2 * u - 6)
                        project_v(0)
                        if g == 0 and prev:
                            need(pe, z_done, n)
                        project_v(1)
                    if g == 3 and prev:
                        need(pe, ln_squared, n)
                        need(pe, v_saved, 8 * n + 8 if cur else 8 * n)
                        for j in range(TILES):
                            last = mm(pO[:, j:j + 1], ln_sq[:, P * j:P * (j + 1)], mean_w[:, 0:1], start=True, stop=True)
                        last.then_inc(var_done, 1)
                    if has(g, 1, prev, cur):
                        need(pe, shifted, u - 1)
                        need(pe, q_rot, u)
                        need(pe, khat_in, 16 * GH * u)
                        scores(0)
                    if g < 3 and cur:
                        lengths()
                    if has(g, 1, prev, cur):
                        scores(1).then_inc(scored, 1)
                    if g == 3 and cur:
                        lengths()
                    if g == 3 and prev:
                        need(pe, rstd_rowed, n)
                        spread(ln_rows[:, 0, :], pO[:]).then_inc(rstd_spread, 1)
                    if has(g, 3, prev, cur):
                        need(pe, placed, u - 2)
                        if g in (1, 2):
                            need(pe, placed_too, 2 * (n - 1) + g)
                        need(pe, v_saved, 2 * u + 2 if cur else 8 * n)
                        if cur:
                            if g < 3:
                                need(pe, by_token, u + 1)
                            else:
                                need(pe, k_prod, u + 1)
                        else:
                            need(pe, k_norm, 4 * n)
                            need(pe, z_done, n)
                        values(0)
                        values(1)
                    if g == 2 and prev:
                        need(pe, wo_in, 16 * ((n - 1) // B + 1))
                        need(pe, o_saved, 8 * n - 1)
                        for i in range(PAIRS // 2):
                            mm(pM[:], wo[:, i, :], heads_out[:, i, :], start=(i == 0), stop=False)
                        need(pe, o_saved, 8 * n)
                    if cur and not (g == 3 and prev):
                        spread_keys()
                    if g == 2 and prev:
                        for i in range(PAIRS // 2, PAIRS):
                            last = mm(pM[:], wo[:, i, :], heads_out[:, i, :], start=False, stop=(i == PAIRS - 1))
                        last.then_inc(o_proj, 1)
                    if g == 2 and cur:
                        need(pe, k_norm, u + 1)
                        project_v(2)
                        if prev:
                            need(pe, z_mid_set, n)
                        project_v(3)
                    if g == 2 and prev:
                        need(pe, z_shifted, n)
                        if cur:
                            need(pe, v_saved, 2 * u + 3)
                        mm(pO[:], mean_w[:], z_shift[:], start=True, stop=True).then_inc(mean_done, 1)
                    if g == 3 and prev:
                        need(pe, ln_done, n)
                        need(pe, wff_in, 32 * ((n - 1) // B + 1))
                        for c, bank in enumerate(GATE_BANK):
                            if c == 0 and cur:
                                need(pe, by_token, u + 1)
                            if c == 2 and cur:
                                need(pe, q_prod, u + 1)
                            f, m = CHUNKS[c]
                            mm(bank[0:m, :], w1[:, FF + f:FF + f + m], ln_aff[:], start=True, stop=True)\
                                .then_inc(gates_up, 1)
                        if cur:
                            spread_keys()
                        need(pe, o_saved, 2 * (u - 3) + 2 if cur else 8 * n)
                        for c, bank in enumerate(UP_BANK):
                            if c == 2 and cur:
                                need(pe, k_norm, u + 1)
                            f, m = CHUNKS[c]
                            mm(bank[0:m, :], w1[:, f:f + m], ln_aff[:], start=True, stop=True).then_inc(values_up, 1)
                        for c in range(NC):
                            need(pe, hidden_set, NC * (n - 1) + c + 1)
                            m = CHUNKS[c][1]
                            last = mm(DOWN_BANK, w2[0:m, c, :], hidden[0:m, c, :], start=(c == 0), stop=(c == NC - 1))
                        last.then_inc(ff_down, 1)

            layer_norms(0)
            pe.wait_ge(consts_in, CONSTS)
            pe.wait_ge(consts_cast, 3)
            emit(lambda n, prev, cur: body(n, prev, cur, 0), pe, 0)
            pe.wait_ge(x_updated, 1)
            layer_norms(1)
            pe.wait_ge(n_done, 2 * B + 1)
            rows_loop(attention, pe)
            pe.wait_ge(a_done, B + 1)
            layer_norms(2)
            emit(lambda n, prev, cur: body(n, prev, cur, 1), pe, ITERS)

        @block.scalar
        def _(act):
            run = nc.scalar.activation
            act.wait_ge(cleared, 7)

            def root_rstd(rows):
                for b in range(rows):
                    run(ln_split[:, b, :, 0:GH], ln_inv[:, b, :].unsqueeze(2).to_broadcast([P, TILES, GH]), ACT.Sqrt)
                return run(ln_rstd[:, 0:rows, :], ln_inv[:, 0:rows, :], ACT.Sqrt)

            def layer_norms(k):
                for b in range(B):
                    need(act, n_centred, B * k + b + 1)
                    run(k_terms[:, b, :], q_terms[:, b, :], ACT.Square).then_inc(n_squared, 1)
                need(act, n_inv, k + 1)
                root_rstd(B).then_inc(n_rstd, 1)

            def attention(b, prev, cur):
                if cur:
                    need(act, a_kqv, b + 1)
                    run(squares[:, 0, :], pS[:, 0, :], ACT.Copy).then_inc(a_k, 1)
                    need(act, a_u, b)
                    run(squares[:, 2, :], pM[:], ACT.Copy).then_inc(a_v, 1)
                    need(act, a_ak, b + 1)
                    run(squares[:, 3, :], pO[:], ACT.Copy).then_inc(a_aks, 1)
                if prev:
                    need(act, a_tr, b)
                    run(k_terms[:, 0:2, :], p4[:, 0:2, :], ACT.Copy).then_inc(a_trs, 1)
                if cur:
                    for i in range(TILES):
                        need(act, a_max, TILES * b + i + 1)
                        run(q_terms[:, i, :], p4[:, i, :], ACT.Exp, bias=row_max[:, i:i + 1]).then_inc(a_exp, 1)

            def shift_in(n, n_ready):
                need(act, z_done, n_ready + 1)
                run(xs[0:D // 2, :], batch(Z, n)[0:D // 2, :], ACT.Copy)
                run(xs[D // 2:D, 1:S], batch(Z, n)[D // 2:D, 0:S - 1], ACT.Copy).then_inc(xs_ready, 1)

            def body(n, prev, cur):
                for g in range(GROUPS):
                    u = 4 * n + g
                    g3 = (g - 3) % GROUPS

                    def save_values(pair):
                        need(act, valued, 2 * (u - 3) + pair + 1)
                        run(heads_out[:, 2 * g3 + pair, :], O_BANK[g][pair], ACT.Copy).then_inc(o_saved, 1)

                    def save_v(c):
                        j, heads = 2 * (c % 2), V_COLS * (g + c // 2)
                        need(act, v_proj, 2 * u + c + 1)
                        run(V[:, j:j + 2, heads:heads + V_COLS], V_BANK[c][:].rearrange("p (j f) -> p j f", j=2),
                            ACT.Copy).then_inc(v_saved, 1)

                    def place(unit, by_vector=0):
                        need(act, transposed, unit + 1)
                        need(act, valued, 2 * unit)
                        for q in range(by_vector, WPT):
                            rows = slice(WIN * q, WIN * (q + 1))
                            run(band[rows, :, :, WIN * q:WIN * (q + 1)], probs_t[rows, :, :, 1, :], ACT.Copy)
                        for q in range(1, WPT):
                            rows = slice(WIN * q, WIN * (q + 1))
                            run(band[WIN * (q - 1):WIN * q, :, :, WIN * q:WIN * (q + 1)],
                                probs_t[rows, :, :, 0, :], ACT.Copy)
                        run(band[P - WIN:P, 0:TILES - 1, :, P:SPAN], probs_t[0:WIN, 1:TILES, :, 0, :], ACT.Copy)\
                            .then_inc(placed, 1)

                    if cur:
                        need(act, k_proj, u + 1)
                        need(act, paired, 2 * u - 1)
                        run(squares[:, 0:2, :], pk, ACT.Square).then_inc(squared, 1)
                    if cur:
                        need(act, q_proj, u + 1)
                        need(act, paired, 2 * u)
                        run(squares[:, 2:4, :], pq, ACT.Square).then_inc(squared, 1)
                    if has(g, 2, prev, cur):
                        need(act, scaled, u - 1)
                        run(probs[:], probs[:], ACT.Exp, scale=QK_SCALE).then_inc(expd, 1)
                    if g < 3 and cur:
                        need(act, valued, 2 * u - 6)
                        save_v(0)
                        save_v(1)
                    if g == 3 and prev:
                        need(act, var_inverted, n)
                        root_rstd(1).then_inc(rstd_set, 1)
                    if g in (1, 2) and has(g, 3, prev, cur):
                        place(u - 3, PLACED_BY_VECTOR)
                    if g == 3 and prev:
                        need(act, ln_scaled, n)
                        need(act, z_done, n)
                        run(ln_aff[:], ln_out[:], ACT.Identity, bias=vff[:, 1:2]).then_inc(ln_done, 1)
                    if cur:
                        need(act, inverted, u + 1)
                        need(act, scaled, u - 1)
                        need(act, k_rowed, u)
                        keys = inv2[:, TILES * GH:].rearrange("p (j h) -> p j h", h=GH)
                        run(k_split[:, :, 0:GH], keys, ACT.Sqrt)
                        run(inv_k[:], keys, ACT.Sqrt)
                        run(inv_q[:, g % 2, :], inv2[:, 0:TILES * GH], ACT.Sqrt).then_inc(rooted, 1)
                    if has(g, 3, prev, cur):
                        if g == 3:
                            need(act, o_proj, n)
                        save_values(0)
                        save_values(1)
                    if g == 2 and cur:
                        place(u - 2)
                        save_v(2)
                        save_v(3)
                    if g == 2 and prev:
                        need(act, centred_set, n)
                        run(ln_sq[:], centred[:], ACT.Square).then_inc(ln_squared, 1)
                    if g == 3 and prev:
                        for c, bank in enumerate(GATE_BANK):
                            m = CHUNKS[c][1]
                            need(act, gates_up, NC * (n - 1) + c + 1)
                            run(gate[0:m, c, :], bank[0:m, :], ACT.Gelu, bias=vff[0:m, 3 + NC + c:4 + NC + c])\
                                .then_inc(gelu_done, 1)
                    if g == 3 and cur:
                        need(act, v_proj, 2 * u + 2)
                        shift_in(n + 1, n - 1)
                        place(u - 2)

            layer_norms(0)
            act.wait_ge(n_done, B + 1)
            shift_in(0, 0)
            emit(body, act, 0)
            layer_norms(1)
            rows_loop(attention, act)
            layer_norms(2)
            act.wait_ge(n_done, 3 * B + 1)
            shift_in(ITERS, ITERS)
            emit(body, act, ITERS)

        @block.vector
        def _(dve):
            v = nc.vector
            v.memset(xs[:], 0.0).then_inc(cleared, 1)
            v.memset(z_shift[:], 0.0).then_inc(cleared, 1)
            v.memset(mean_w[:], 1.0 / D).then_inc(cleared, 1)
            v.memset(k_split[:].bitcast(F32), 0.0).then_inc(cleared, 1)
            v.memset(ln_split[:].bitcast(F32), 0.0).then_inc(cleared, 1)
            for i, primed in enumerate((z_done, n_done, a_done)):
                v.memset(primer[:, i:i + 1], 0.0).then_inc(primed, 1)
            dve.wait_ge(state_in, 2 * 16)
            v.tensor_copy(row_sel[:].rearrange("p q m -> p (q m)"), squares[:, 2, :]).then_inc(consts_cast, 1)
            dve.wait_ge(cleared, 7)

            def rows_of(split, value, rows, turned, low, turned_, count):
                v.tensor_tensor(split[:, :, GH:2 * GH], value, split[:, :, 0:GH].bitcast(F32), ALU.subtract)\
                    .then_inc(low, 1)
                need(dve, low, count)
                v.transpose(turned, split.bitcast(F32).rearrange("p j r -> p (j r)")).then_inc(turned_, 1)
                need(dve, turned_, count)
                return v.tensor_copy(rows, turned)

            def layer_norms(k):
                for b in range(B):
                    need(dve, n_mean, B * k + b + 1)
                    v.tensor_tensor(q_terms[:, b, :], X[:, b, :], p4[:, b, :], ALU.subtract).then_inc(n_centred, 1)
                need(dve, n_var, k + 1)
                v.tensor_scalar(ln_var[:].rearrange("p b j -> p (b j)"), pM[:, 0:B * TILES], LN_EPS, None, ALU.add)\
                    .then_inc(n_eps, 1)
                need(dve, n_eps, k + 1)
                v.reciprocal(ln_inv[:], ln_var[:]).then_inc(n_inv, 1)
                need(dve, n_rstd, k + 1)
                rows_of(ln_split[:].rearrange("p b j r -> p (b j) r"),
                        ln_rstd[:].rearrange("p b j -> p (b j)").unsqueeze(2).to_broadcast([P, B * TILES, GH]),
                        ln_rows[:].rearrange("p b r -> p (b r)"), turned[:].rearrange("p b r -> p (b r)"),
                        n_low, n_turned, k + 1).then_inc(n_rowed, 1)
                for b in range(B):
                    need(dve, n_spread, B * k + b + 1)
                    v.tensor_tensor(Z[:, b, :], q_terms[:, b, :], p4[:, b, :], ALU.mult).then_inc(n_done, 1)

            def attention(b, prev, cur):
                if cur:
                    need(dve, a_kqv, b + 1)
                    v.tensor_copy(squares[:, 1, :], pS[:, 1, :]).then_inc(a_q, 1)
                if prev:
                    need(dve, a_tr, b)
                    v.tensor_copy(k_terms[:, 2:4, :], p4[:, 2:4, :]).then_inc(a_trd, 1)
                    need(dve, a_out, b)
                    v.tensor_tensor(batch(X, b - 1), batch(X, b - 1), pM[:], ALU.add).then_inc(a_done, 1)
                if cur:
                    need(dve, a_u, b + 1)
                    v.tensor_copy(sumsq[:, 0, :], pS[:, 0, :]).then_inc(a_us, 1)
                    for i in range(TILES):
                        need(dve, a_scores, TILES * b + i + 1)
                        v.tensor_reduce(row_max[:, i:i + 1], p4[:, i, :], AX_X, ALU.max, negate=True).then_inc(a_max, 1)
                    for i in range(TILES):
                        need(dve, a_exp, TILES * b + i + 1)
                        last = v.reduce_sum(row_sum[:, i:i + 1], q_terms[:, i, :], AX_X)
                    last.then_inc(a_sum, 1)
                    need(dve, a_sum, b + 1)
                    v.reciprocal(inv_sum[:, 0:TILES], row_sum[:, 0:TILES]).then_inc(a_isum, 1)
                    need(dve, a_isum, b + 1)
                    for i in range(TILES):
                        v.tensor_scalar(q_terms[:, i, :], q_terms[:, i, :], inv_sum[:, i:i + 1], None, ALU.mult)\
                            .then_inc(a_norm, 1)

            def body(n, prev, cur, st):
                if cur:
                    need(dve, k_prod, 4 * n)
                    layer = n // B - LAYERS * st
                    v.tensor_copy(vqk[:], vecs[:, bass.ds(layer, 1), 0:4].rearrange("p a c -> p (a c)"))\
                        .then_inc(vqk_set, 1)
                    need(dve, vqk_set, n + 1)
                for g in range(GROUPS):
                    u = 4 * n + g

                    def sum_rows():
                        need(dve, expd, u - 1)
                        v.reduce_sum(row_sum[:], probs[:], AX_X).then_inc(rows_summed, 1)
                        need(dve, rows_summed, u - 1)
                        v.reciprocal(inv_sum[:], row_sum[:]).then_inc(sums_inverted, 1)

                    def transpose_probs():
                        need(dve, normed, u - 1)
                        need(dve, placed, u - 2)
                        if g in (1, 2) and has(g, 3, prev, cur):
                            need(dve, placed_too, 2 * (n - 1) + g)
                        v.transpose(probs_t[:].rearrange("p j h b t -> p (j h b t)"),
                                    probs[:].rearrange("p r s -> p (r s)")).then_inc(transposed, 1)

                    scores = pS[:].rearrange("p b (r s) -> p (b r) s", s=2 * WIN)

                    def subtract_max():
                        need(dve, maxed, u)
                        need(dve, transposed, u - 1)
                        v.tensor_tensor(probs[:], scores, row_max[:].unsqueeze(2).to_broadcast([P, TILES * GH, 2 * WIN]),
                                        ALU.subtract).then_inc(shifted, 1)

                    def rows_of_keys():
                        need(dve, rooted, u + 1)
                        need(dve, spread_k, u)
                        rows_of(k_split[:], inv_k[:], k_rows[:], turned[:, 0, :], k_low, k_turned, u + 1).then_inc(k_rowed, 1)

                    def terms(dst, src, vcol, cos, sin, which=(0, 1, 2, 3)):
                        for i in which:
                            half, table = ((0, cos), (1, sin), (1, cos), (0, sin))[i]
                            last = v.scalar_tensor_tensor(out=dst[:, i, :], in0=src[:, half, :],
                                                          scalar=vqk[:, vcol + half:vcol + half + 1], in1=table,
                                                          op0=ALU.mult, op1=ALU.mult)
                        return last

                    if cur:
                        need(dve, squared, 2 * u + 1)
                        need(dve, k_rot, u)
                        terms(k_terms, pk, 2, ck, sk).then_inc(k_prod, 1)
                    if g == 3 and prev:
                        need(dve, var_done, n)
                        v.tensor_scalar(ln_var[:, 0, :], pO[:, 0:TILES], LN_EPS, None, ALU.add).then_inc(var_eps, 1)
                        need(dve, var_eps, n)
                        v.reciprocal(ln_inv[:, 0, :], ln_var[:, 0, :]).then_inc(var_inverted, 1)
                    if cur:
                        need(dve, squared, 2 * u + 2)
                        need(dve, q_rot, u)
                        terms(q_terms, pq, 0, cq, sq_, (0, 1))
                    if g == 3 and prev:
                        need(dve, rstd_set, n)
                        rows_of(ln_split[:, 0, :, :], ln_rstd[:, 0, :].unsqueeze(2).to_broadcast([P, TILES, GH]),
                                ln_rows[:, 0, :], turned[:, 0, :], rstd_low, rstd_turned, n).then_inc(rstd_rowed, 1)
                    if g in (1, 2) and has(g, 3, prev, cur):
                        need(dve, transposed, u - 2)
                        need(dve, valued, 2 * (u - 3))
                        for q in range(PLACED_BY_VECTOR):
                            rows = slice(WIN * q, WIN * (q + 1))
                            last = v.tensor_copy(band[rows, :, :, WIN * q:WIN * (q + 1)], probs_t[rows, :, :, 1, :])
                        last.then_inc(placed_too, 1)
                    if has(g, 2, prev, cur):
                        sum_rows()
                    if g == 3 and prev:
                        need(dve, rstd_spread, n)
                        v.scalar_tensor_tensor(out=ln_out[:], in0=centred[:], scalar=vff[:, 0:1], in1=pO[:],
                                               op0=ALU.mult, op1=ALU.mult).then_inc(ln_scaled, 1)
                    if cur:
                        need(dve, summed, u + 1)
                        need(dve, clamped, u)
                        v.transpose(tok_sums[:].rearrange("p a b -> p (a b)"), pM[:, 0:2 * P]).then_inc(by_token, 1)
                        need(dve, by_token, u + 1)
                        need(dve, inverted, u)
                        v.tensor_scalar(norm2[:].rearrange("p (a h) -> p a h", h=GH), tok_sums[:, :, 0:GH],
                                        NORM_EPS ** 2, None, ALU.max).then_inc(clamped, 1)
                        need(dve, clamped, u + 1)
                        need(dve, rooted, u)
                        v.reciprocal(inv2[:], norm2[:]).then_inc(inverted, 1)
                        terms(q_terms, pq, 0, cq, sq_, (2, 3)).then_inc(q_prod, 1)
                        rows_of_keys()
                    if has(g, 1, prev, cur):
                        need(dve, scored, u)
                        v.reduce_max(row_max[:], scores, AX_X).then_inc(maxed, 1)
                    if g > 1 and has(g, 2, prev, cur):
                        transpose_probs()
                    if cur:
                        need(dve, spread_k, u + 1)
                        need(dve, k_rot, u + 1)
                        need(dve, khat_in, 16 * GH * u)
                        v.tensor_tensor(k_normed[:], k_rotated[:], K_BANK[g].unsqueeze(1).to_broadcast([P, 2, S]),
                                        ALU.mult).then_inc(k_norm, 1)
                    if g < 2 and has(g, 2, prev, cur):
                        transpose_probs()
                    if g < 3 and has(g, 1, prev, cur):
                        subtract_max()
                    if g == 2 and prev:
                        need(dve, z_done, n)
                        layer = (n - 1) // B - LAYERS * st
                        v.tensor_copy(vff[:], vecs[:, bass.ds(layer, 1), 4:].rearrange("p a c -> p (a c)"))\
                            .then_inc(vff_set, 1)
                        need(dve, o_proj, n)
                        v.tensor_tensor(z_mid[:], batch(Z, n - 1), pM[:], ALU.add).then_inc(z_mid_set, 1)
                        need(dve, z_mid_set, n)
                        v.tensor_copy(z_shift[0:D // 2, :], z_mid[0:D // 2, :])
                        v.tensor_copy(z_shift[D // 2:D, 1:S], z_mid[D // 2:D, 0:S - 1]).then_inc(z_shifted, 1)
                        need(dve, z_shifted, n)
                        need(dve, mean_done, n)
                        v.tensor_tensor(centred[:], z_shift[:], pO[:], ALU.subtract).then_inc(centred_set, 1)
                    if g == 3 and prev:
                        need(dve, vff_set, n)
                        for c, bank in enumerate(UP_BANK):
                            m = CHUNKS[c][1]
                            need(dve, gelu_done, NC * (n - 1) + c + 1)
                            need(dve, values_up, NC * (n - 1) + c + 1)
                            v.scalar_tensor_tensor(out=hidden[0:m, c, :], in0=bank[0:m, :], scalar=vff[0:m, 3 + c:4 + c],
                                                   in1=gate[0:m, c, :], op0=ALU.add, op1=ALU.mult)\
                                .then_inc(hidden_set, 1)
                    if g == 3 and has(g, 1, prev, cur):
                        subtract_max()
                    if g == 3 and prev:
                        need(dve, ff_down, n)
                        v.scalar_tensor_tensor(out=batch(Z, n - 1), in0=DOWN_BANK, scalar=vff[:, 2:3], in1=z_mid[:],
                                               op0=ALU.add, op1=ALU.add).then_inc(z_done, 1)

            layer_norms(0)
            dve.wait_ge(consts_in, CONSTS)
            v.tensor_copy(identity16[:], identity[:]).then_inc(consts_cast, 1)
            v.tensor_copy(mask16[:], squares[:, 0:2, :]).then_inc(consts_cast, 1)
            dve.wait_ge(n_done, B + 1)
            emit(lambda n, prev, cur: body(n, prev, cur, 0), dve, 0)
            dve.wait_ge(z_done, ITERS + 1)
            v.scalar_tensor_tensor(out=X[:], in0=Z[:], scalar=0.5, in1=X[:], op0=ALU.mult, op1=ALU.add)\
                .then_inc(x_updated, 1)
            dve.wait_ge(x_updated, 1)
            layer_norms(1)
            dve.wait_ge(n_done, 2 * B + 1)
            rows_loop(attention, dve)
            dve.wait_ge(a_done, B + 1)
            layer_norms(2)
            dve.wait_ge(n_done, 3 * B + 1)
            emit(lambda n, prev, cur: body(n, prev, cur, 1), dve, ITERS)
            dve.wait_ge(z_done, 2 * ITERS + 1)
            v.scalar_tensor_tensor(out=X[:], in0=Z[:], scalar=0.5, in1=X[:], op0=ALU.mult, op1=ALU.add)\
                .then_inc(x_updated, 1)

        @block.gpsimd
        def _(pool):
            tt = nc.gpsimd.tensor_tensor

            def body(n, prev, cur):
                for g in range(GROUPS):
                    u = 4 * n + g
                    if has(g, 2, prev, cur):
                        need(pool, shifted, u - 1)
                        need(pool, rooted, u - 1)
                        tt(probs[:], probs[:], inv_q[:, g % 2, :].unsqueeze(2).to_broadcast([P, TILES * GH, 2 * WIN]),
                           ALU.mult).then_inc(scaled, 1)
                    if cur:
                        for i, qk in enumerate((1, 0)):
                            need(pool, squared, 2 * u + i + 1)
                            need(pool, summed, u)
                            tt(sumsq[:, qk, :], squares[:, 2 * i, :], squares[:, 2 * i + 1, :], ALU.add)\
                                .then_inc(paired, 1)
                    if cur:
                        need(pool, k_prod, u + 1)
                        need(pool, k_norm, u)
                        tt(k_rotated[:, 0, :], k_terms[:, 0, :], k_terms[:, 1, :], ALU.subtract)
                        tt(k_rotated[:, 1, :], k_terms[:, 2, :], k_terms[:, 3, :], ALU.add).then_inc(k_rot, 1)
                    if has(g, 2, prev, cur):
                        need(pool, sums_inverted, u - 1)
                        tt(probs[:], probs[:], inv_sum[:].unsqueeze(2).to_broadcast([P, TILES * GH, 2 * WIN]), ALU.mult)\
                            .then_inc(normed, 1)
                    if cur:
                        need(pool, q_prod, u + 1)
                        need(pool, scored, u - 1)
                        qr = q_rotated[:, g % 2, :, :]
                        tt(qr[:, 0, :], q_terms[:, 0, :], q_terms[:, 1, :], ALU.subtract)
                        tt(qr[:, 1, :], q_terms[:, 2, :], q_terms[:, 3, :], ALU.add).then_inc(q_rot, 1)

            nc.gpsimd.memset(khat[:], 0.0).then_inc(cleared, 1)
            nc.gpsimd.memset(band[:], 0.0).then_inc(cleared, 1)
            emit(body, pool, 0)
            pool.wait_ge(a_done, B + 1)
            emit(body, pool, ITERS)


def kernel(**inputs):
    import numpy as np
    import concourse.bacc as bacc
    from concourse.bass_utils import run_bass_kernel_spmd

    a = {k: np.asarray(x) for k, x in inputs.items()}
    f = lambda name: a["L0_ffn_" + name]
    w = f("Wqkv").reshape(LAYERS, D, 3, GROUPS, GH, 2, HALF)
    vec = np.zeros((P, LAYERS, VEC), np.float32)
    for c, name in ((0, "q_scale"), (2, "k_scale")):
        halves = f(name).reshape(LAYERS, 2, HALF).transpose(2, 0, 1)
        vec[:, :, c:c + 2] = np.tile(halves, (GH, 1, 1))
    vec[:, :, 4], vec[:, :, 5], vec[:, :, 6] = f("ln_g").T, f("ln_b").T, f("b2").T
    b1 = f("b1")
    w2 = np.zeros((LAYERS, P, NC, D), np.float32)
    for c, (at, m) in enumerate(CHUNKS):
        vec[0:m, :, 7 + c] = b1[:, at:at + m].T
        vec[0:m, :, 7 + NC + c] = b1[:, FF + at:FF + at + m].T
        w2[:, 0:m, c] = f("W2")[:, at:at + m]

    half = np.arange(0, DH, 2, dtype=np.float32)
    inv_freq = (1.0 / np.float32(10000.0) ** (half / np.float32(DH))).astype(np.float32)
    t = np.arange(S, dtype=np.float32)
    angle = (inv_freq[:, None] * t[None, :]).astype(np.float32)
    base = ((half + np.float32(0.4 * DH)) / np.float32(1.4 * DH)).astype(np.float32)
    scale = (base[:, None] ** ((t - S // 2) / (WIN // 2))[None, :]).astype(np.float32)
    cos, sin = np.cos(angle), np.sin(angle)
    rot = np.stack([cos * scale, sin * scale, cos * (1 / scale), sin * (1 / scale)], 1).astype(np.float32)
    rot = np.tile(rot, (GH, 1, 1))
    r, s = np.arange(P)[:, None] % WIN, np.arange(2 * WIN)[None, :]
    allowed = (s >= r) & (s <= r + WIN)
    mask = np.where(allowed, 0.0, MASKED).astype(np.float32)[:, None, None, :]
    mask = np.broadcast_to(mask, (P, TILES, GH, 2 * WIN)).copy()
    mask[0:WIN, 0, :, 0:WIN] = MASKED
    sel = (np.arange(P)[:, None] // HALF == np.arange(WIN)[None, :]).astype(np.float32)
    row = np.arange(P)[:, None] % WIN
    spread_sel = (row < 2 * GH) & (row % GH == np.arange(P)[None, :] // HALF)
    spread_sel = np.stack([spread_sel & (np.arange(P)[:, None] // WIN == q) for q in range(WPT)], 1)

    arrays = {
        "x_t": a["L0_attn_x"].transpose(2, 0, 1),
        "w_qk": w[:, :, 0:2].transpose(0, 3, 1, 2, 5, 4, 6).reshape(LAYERS, GROUPS, D, 4 * P),
        "w_v": f("Wqkv")[:, :, 2 * HEADS * DH:],
        "w_o": f("Wo").reshape(LAYERS, PAIRS, P, D).transpose(0, 2, 1, 3).reshape(LAYERS, P, PAIRS * D),
        "w_1": f("W1"),
        "w_2": w2.reshape(LAYERS, P, NC * D),
        "vec": vec,
        "rot": rot,
        "mask": mask.reshape(P, 2, S),
        "ident": np.eye(P, dtype=np.float32),
        "a_w": np.concatenate([a["L0_attn_W" + c].T for c in "kqvab"], 1),
        "sel": sel,
        "spread_sel": spread_sel.reshape(P, WPT * P).astype(np.float32),
    }
    arrays = {k: np.ascontiguousarray(x) for k, x in arrays.items()}
    nc = bacc.Bacc("TRN2", target_bir_lowering=False, num_devices=1)
    args = {k: nc.dram_tensor(k + "_dram", x.shape, F32, kind="ExternalInput").ap() for k, x in arrays.items()}
    out = nc.dram_tensor("out_dram", (P, B, S), F32, kind="ExternalOutput").ap()
    macaron(nc, **args, out=out)
    r = run_bass_kernel_spmd(nc, [{k + "_dram": x for k, x in arrays.items()}], core_ids=[0])
    return np.ascontiguousarray(r.results[0]["out_dram"].transpose(1, 2, 0))
```
